# Optimizing a Trainium2 kernel written in Bass

```python
import numpy as np
import jax
import jax.numpy as jnp

def _softmax(x, axis=-1):
    return jax.nn.softmax(x, axis=axis)

def _gelu(x):
    return jax.nn.gelu(x, approximate=True)

def _silu(x):
    return jax.nn.silu(x)

def _sigmoid(x):
    return jax.nn.sigmoid(x)

def _layernorm(x, axis=-1, eps=1e-05):
    m = jnp.mean(x, axis=axis, keepdims=True)
    v = jnp.var(x, axis=axis, keepdims=True)
    return (x - m) / jnp.sqrt(v + eps)

def _scatter_add(tgt, idx, src, axis=0):
    return tgt.at[idx].add(src)

def _segment_sum(src, seg, n):
    return jax.ops.segment_sum(src, seg, n)
kernel_name = 'mk_dlrm_tower_d1_rec_r8_571653'

def setup_inputs(seed: int=0):
    np.random.seed(seed)
    _w = jnp.asarray

    def _rec_inputs():
        import jax
        import jax.numpy as jnp
        _tk = jax.random.key(seed)
        dense_ctx = jax.random.normal(jax.random.fold_in(_tk, 190), (2048, 16), jnp.float32)
        ids = jnp.stack([jax.random.randint(jax.random.fold_in(_tk, 200 + f), (2048,), 0, v, jnp.int32) for f, v in enumerate([1000, 125000, 12500, 1250, 1000, 1250, 125000, 125000, 1250, 1250, 1000, 125000, 1250, 1000, 125000, 125000, 1000, 125000, 1250, 12500, 1250, 1250, 1250, 12500, 12500, 1250, 1000, 1250, 1000, 1000, 12500, 1250, 12500, 1250, 1000, 1000, 1000, 1250, 1250])], axis=1)
        tbl_0 = 0.05 * jax.random.normal(jax.random.fold_in(_tk, 500 + 0), (1000, 32), jnp.float32)
        tbl_1 = 0.05 * jax.random.normal(jax.random.fold_in(_tk, 500 + 1), (125000, 32), jnp.float32)
        tbl_2 = 0.05 * jax.random.normal(jax.random.fold_in(_tk, 500 + 2), (12500, 32), jnp.float32)
        tbl_3 = 0.05 * jax.random.normal(jax.random.fold_in(_tk, 500 + 3), (1250, 32), jnp.float32)
        tbl_4 = 0.05 * jax.random.normal(jax.random.fold_in(_tk, 500 + 4), (1000, 32), jnp.float32)
        tbl_5 = 0.05 * jax.random.normal(jax.random.fold_in(_tk, 500 + 5), (1250, 32), jnp.float32)
        tbl_6 = 0.05 * jax.random.normal(jax.random.fold_in(_tk, 500 + 6), (125000, 32), jnp.float32)
        tbl_7 = 0.05 * jax.random.normal(jax.random.fold_in(_tk, 500 + 7), (125000, 32), jnp.float32)
        tbl_8 = 0.05 * jax.random.normal(jax.random.fold_in(_tk, 500 + 8), (1250, 32), jnp.float32)
        tbl_9 = 0.05 * jax.random.normal(jax.random.fold_in(_tk, 500 + 9), (1250, 32), jnp.float32)
        tbl_10 = 0.05 * jax.random.normal(jax.random.fold_in(_tk, 500 + 10), (1000, 32), jnp.float32)
        tbl_11 = 0.05 * jax.random.normal(jax.random.fold_in(_tk, 500 + 11), (125000, 32), jnp.float32)
        tbl_12 = 0.05 * jax.random.normal(jax.random.fold_in(_tk, 500 + 12), (1250, 32), jnp.float32)
        tbl_13 = 0.05 * jax.random.normal(jax.random.fold_in(_tk, 500 + 13), (1000, 32), jnp.float32)
        tbl_14 = 0.05 * jax.random.normal(jax.random.fold_in(_tk, 500 + 14), (125000, 32), jnp.float32)
        tbl_15 = 0.05 * jax.random.normal(jax.random.fold_in(_tk, 500 + 15), (125000, 32), jnp.float32)
        tbl_16 = 0.05 * jax.random.normal(jax.random.fold_in(_tk, 500 + 16), (1000, 32), jnp.float32)
        tbl_17 = 0.05 * jax.random.normal(jax.random.fold_in(_tk, 500 + 17), (125000, 32), jnp.float32)
        tbl_18 = 0.05 * jax.random.normal(jax.random.fold_in(_tk, 500 + 18), (1250, 32), jnp.float32)
        tbl_19 = 0.05 * jax.random.normal(jax.random.fold_in(_tk, 500 + 19), (12500, 32), jnp.float32)
        tbl_20 = 0.05 * jax.random.normal(jax.random.fold_in(_tk, 500 + 20), (1250, 32), jnp.float32)
        tbl_21 = 0.05 * jax.random.normal(jax.random.fold_in(_tk, 500 + 21), (1250, 32), jnp.float32)
        tbl_22 = 0.05 * jax.random.normal(jax.random.fold_in(_tk, 500 + 22), (1250, 32), jnp.float32)
        tbl_23 = 0.05 * jax.random.normal(jax.random.fold_in(_tk, 500 + 23), (12500, 32), jnp.float32)
        tbl_24 = 0.05 * jax.random.normal(jax.random.fold_in(_tk, 500 + 24), (12500, 32), jnp.float32)
        tbl_25 = 0.05 * jax.random.normal(jax.random.fold_in(_tk, 500 + 25), (1250, 32), jnp.float32)
        tbl_26 = 0.05 * jax.random.normal(jax.random.fold_in(_tk, 500 + 26), (1000, 32), jnp.float32)
        tbl_27 = 0.05 * jax.random.normal(jax.random.fold_in(_tk, 500 + 27), (1250, 32), jnp.float32)
        tbl_28 = 0.05 * jax.random.normal(jax.random.fold_in(_tk, 500 + 28), (1000, 32), jnp.float32)
        tbl_29 = 0.05 * jax.random.normal(jax.random.fold_in(_tk, 500 + 29), (1000, 32), jnp.float32)
        tbl_30 = 0.05 * jax.random.normal(jax.random.fold_in(_tk, 500 + 30), (12500, 32), jnp.float32)
        tbl_31 = 0.05 * jax.random.normal(jax.random.fold_in(_tk, 500 + 31), (1250, 32), jnp.float32)
        tbl_32 = 0.05 * jax.random.normal(jax.random.fold_in(_tk, 500 + 32), (12500, 32), jnp.float32)
        tbl_33 = 0.05 * jax.random.normal(jax.random.fold_in(_tk, 500 + 33), (1250, 32), jnp.float32)
        tbl_34 = 0.05 * jax.random.normal(jax.random.fold_in(_tk, 500 + 34), (1000, 32), jnp.float32)
        tbl_35 = 0.05 * jax.random.normal(jax.random.fold_in(_tk, 500 + 35), (1000, 32), jnp.float32)
        tbl_36 = 0.05 * jax.random.normal(jax.random.fold_in(_tk, 500 + 36), (1000, 32), jnp.float32)
        tbl_37 = 0.05 * jax.random.normal(jax.random.fold_in(_tk, 500 + 37), (1250, 32), jnp.float32)
        tbl_38 = 0.05 * jax.random.normal(jax.random.fold_in(_tk, 500 + 38), (1250, 32), jnp.float32)
        _rk = jax.random.fold_in(_tk, 7)
        W_top1 = 0.0693375 * jax.random.normal(jax.random.fold_in(_tk, 801), (208, 512), jnp.float32)
        W_top2 = 0.0441942 * jax.random.normal(jax.random.fold_in(_tk, 802), (512, 256), jnp.float32)
        W_top3 = 0.0625 * jax.random.normal(jax.random.fold_in(_tk, 803), (256, 1), jnp.float32)
        b_top1 = jnp.zeros((512,), jnp.float32)
        b_top2 = jnp.zeros((256,), jnp.float32)
        return (dense_ctx, ids, tbl_0, tbl_1, tbl_2, tbl_3, tbl_4, tbl_5, tbl_6, tbl_7, tbl_8, tbl_9, tbl_10, tbl_11, tbl_12, tbl_13, tbl_14, tbl_15, tbl_16, tbl_17, tbl_18, tbl_19, tbl_20, tbl_21, tbl_22, tbl_23, tbl_24, tbl_25, tbl_26, tbl_27, tbl_28, tbl_29, tbl_30, tbl_31, tbl_32, tbl_33, tbl_34, tbl_35, tbl_36, tbl_37, tbl_38, W_top1, b_top1, W_top2, b_top2, W_top3)
    dense_ctx, ids, tbl_0, tbl_1, tbl_2, tbl_3, tbl_4, tbl_5, tbl_6, tbl_7, tbl_8, tbl_9, tbl_10, tbl_11, tbl_12, tbl_13, tbl_14, tbl_15, tbl_16, tbl_17, tbl_18, tbl_19, tbl_20, tbl_21, tbl_22, tbl_23, tbl_24, tbl_25, tbl_26, tbl_27, tbl_28, tbl_29, tbl_30, tbl_31, tbl_32, tbl_33, tbl_34, tbl_35, tbl_36, tbl_37, tbl_38, W_top1, b_top1, W_top2, b_top2, W_top3 = _rec_inputs()

    def _L0_rec_setup():
        import jax, jax.numpy as jnp
        import numpy as np
        LAYER_SIZES = (128, 128)

        def _cin_layer(h0, h, W):
            F0, Fi = (h0.shape[1], h.shape[1])
            K = W.shape[1]
            Wr = W.reshape(F0, Fi, K)
            return jnp.einsum('bid,bjd,ijk->bkd', h0, h, Wr)
        key = jax.random.key(seed)
        k1, k2, k3 = jax.random.split(key, 3)
        B, F0, D = (256, 39, 32)
        F1 = LAYER_SIZES[0] // 2
        x = jax.random.normal(k1, (B, F0, D), dtype=jnp.float32)
        W1 = jax.random.normal(k2, (F0 * F0, LAYER_SIZES[0]), dtype=jnp.float32) * 0.05
        W2 = jax.random.normal(k3, (F0 * F1, LAYER_SIZES[1]), dtype=jnp.float32) * 0.05
        return {'x': x, 'W1': W1, 'W2': W2}
    _L0_rec_all = _L0_rec_setup()
    _L0_rec_in = {k: v for k, v in _L0_rec_all.items() if k in ('W1', 'W2')}
    del _L0_rec_all
    return {'dense_ctx': dense_ctx, 'ids': ids, 'tbl_0': tbl_0, 'tbl_1': tbl_1, 'tbl_2': tbl_2, 'tbl_3': tbl_3, 'tbl_4': tbl_4, 'tbl_5': tbl_5, 'tbl_6': tbl_6, 'tbl_7': tbl_7, 'tbl_8': tbl_8, 'tbl_9': tbl_9, 'tbl_10': tbl_10, 'tbl_11': tbl_11, 'tbl_12': tbl_12, 'tbl_13': tbl_13, 'tbl_14': tbl_14, 'tbl_15': tbl_15, 'tbl_16': tbl_16, 'tbl_17': tbl_17, 'tbl_18': tbl_18, 'tbl_19': tbl_19, 'tbl_20': tbl_20, 'tbl_21': tbl_21, 'tbl_22': tbl_22, 'tbl_23': tbl_23, 'tbl_24': tbl_24, 'tbl_25': tbl_25, 'tbl_26': tbl_26, 'tbl_27': tbl_27, 'tbl_28': tbl_28, 'tbl_29': tbl_29, 'tbl_30': tbl_30, 'tbl_31': tbl_31, 'tbl_32': tbl_32, 'tbl_33': tbl_33, 'tbl_34': tbl_34, 'tbl_35': tbl_35, 'tbl_36': tbl_36, 'tbl_37': tbl_37, 'tbl_38': tbl_38, 'W_top1': W_top1, 'b_top1': b_top1, 'W_top2': W_top2, 'b_top2': b_top2, 'W_top3': W_top3, 'L0_rec_W1': _L0_rec_in['W1'], 'L0_rec_W2': _L0_rec_in['W2']}

def reference(dense_ctx, ids, tbl_0, tbl_1, tbl_2, tbl_3, tbl_4, tbl_5, tbl_6, tbl_7, tbl_8, tbl_9, tbl_10, tbl_11, tbl_12, tbl_13, tbl_14, tbl_15, tbl_16, tbl_17, tbl_18, tbl_19, tbl_20, tbl_21, tbl_22, tbl_23, tbl_24, tbl_25, tbl_26, tbl_27, tbl_28, tbl_29, tbl_30, tbl_31, tbl_32, tbl_33, tbl_34, tbl_35, tbl_36, tbl_37, tbl_38, W_top1, b_top1, W_top2, b_top2, W_top3, L0_rec_W1, L0_rec_W2):
    import jax
    import jax.numpy as jnp

    def _L0_rec_ref(x, W1, W2):
        import jax, jax.numpy as jnp
        import numpy as np
        LAYER_SIZES = (128, 128)

        def _cin_layer(h0, h, W):
            F0, Fi = (h0.shape[1], h.shape[1])
            K = W.shape[1]
            Wr = W.reshape(F0, Fi, K)
            return jnp.einsum('bid,bjd,ijk->bkd', h0, h, Wr)
        conv1 = _cin_layer(x, x, W1)
        half = LAYER_SIZES[0] // 2
        hidden1 = conv1[:, :half, :]
        final1 = conv1[:, half:, :]
        conv2 = _cin_layer(x, hidden1, W2)
        final = jnp.concatenate([final1, conv2], axis=1)
        return jnp.sum(final, axis=2)
    e = jnp.stack([tbl_0[ids[:, 0]], tbl_1[ids[:, 1]], tbl_2[ids[:, 2]], tbl_3[ids[:, 3]], tbl_4[ids[:, 4]], tbl_5[ids[:, 5]], tbl_6[ids[:, 6]], tbl_7[ids[:, 7]], tbl_8[ids[:, 8]], tbl_9[ids[:, 9]], tbl_10[ids[:, 10]], tbl_11[ids[:, 11]], tbl_12[ids[:, 12]], tbl_13[ids[:, 13]], tbl_14[ids[:, 14]], tbl_15[ids[:, 15]], tbl_16[ids[:, 16]], tbl_17[ids[:, 17]], tbl_18[ids[:, 18]], tbl_19[ids[:, 19]], tbl_20[ids[:, 20]], tbl_21[ids[:, 21]], tbl_22[ids[:, 22]], tbl_23[ids[:, 23]], tbl_24[ids[:, 24]], tbl_25[ids[:, 25]], tbl_26[ids[:, 26]], tbl_27[ids[:, 27]], tbl_28[ids[:, 28]], tbl_29[ids[:, 29]], tbl_30[ids[:, 30]], tbl_31[ids[:, 31]], tbl_32[ids[:, 32]], tbl_33[ids[:, 33]], tbl_34[ids[:, 34]], tbl_35[ids[:, 35]], tbl_36[ids[:, 36]], tbl_37[ids[:, 37]], tbl_38[ids[:, 38]]], axis=1)
    z = _L0_rec_ref(e, L0_rec_W1, L0_rec_W2)
    z = z.reshape(z.shape[0], -1)
    h = jnp.concatenate([z, dense_ctx], axis=1)
    h = jnp.maximum(h @ W_top1 + b_top1, 0.0)
    h = jnp.maximum(h @ W_top2 + b_top2, 0.0)
    y = h @ W_top3
    return y

_drawn_inputs = setup_inputs


def setup_inputs(seed=0):
    import zlib

    import numpy as np

    out = dict(_drawn_inputs(seed))
    spreads = {'b_top1': (0.0, 0.1), 'b_top2': (0.0, 0.1)}
    factors = {'tbl_0': 4.712,
     'tbl_1': 4.87,
     'tbl_2': 4.895,
     'tbl_3': 4.989,
     'tbl_4': 4.789,
     'tbl_5': 4.584,
     'tbl_6': 4.783,
     'tbl_7': 4.625,
     'tbl_8': 4.775,
     'tbl_9': 4.826,
     'tbl_10': 5.116,
     'tbl_11': 4.365,
     'tbl_12': 4.837,
     'tbl_13': 4.696,
     'tbl_14': 4.264,
     'tbl_15': 4.746,
     'tbl_16': 4.533,
     'tbl_17': 4.611,
     'tbl_18': 4.885,
     'tbl_19': 5.092,
     'tbl_20': 4.918,
     'tbl_21': 4.802,
     'tbl_22': 5.061,
     'tbl_23': 5.1,
     'tbl_24': 4.599,
     'tbl_25': 4.741,
     'tbl_26': 4.828,
     'tbl_27': 4.611,
     'tbl_28': 4.565,
     'tbl_29': 4.762,
     'tbl_30': 4.243,
     'tbl_31': 4.621,
     'tbl_32': 4.955,
     'tbl_33': 4.468,
     'tbl_34': 5.022,
     'tbl_35': 4.807,
     'tbl_36': 4.967,
     'tbl_37': 4.706,
     'tbl_38': 4.645,
     'L0_rec_W2': 5.653}
    for name, (base, spread) in spreads.items():
        noise = np.random.default_rng([zlib.crc32(name.encode()), seed]).standard_normal(out[name].shape)
        drawn = base * np.exp(spread * noise) if base else spread * noise
        out[name] = jnp.asarray(drawn.astype(out[name].dtype))
    for name, factor in factors.items():
        out[name] = (out[name] * factor).astype(out[name].dtype)
    return out
```

```python
from contextlib import ExitStack

import concourse.bass as bass
from concourse import mybir

F32 = mybir.dt.float32
BF16 = mybir.dt.bfloat16
I32 = mybir.dt.int32
ALU = mybir.AluOpType
ACT = mybir.ActivationFunctionType

P = 128
F = 39
D = 32
Q = 4
HID = 64
FIN1 = 64
CONV2 = 128
B = 2048
TILES = B // P
PAIRS = TILES // 2
PLACES = 32
HALF = PLACES // 2
COLS = HALF * Q * D
NPAIR = F * (F + 1) // 2
FULL = NPAIR // P
REST = NPAIR - FULL * P
STEPS = FULL + 1
W1T = -(-F * F // P)
W1LAST = F * F - (W1T - 1) * P
FH = -(-F // 2)
GS = HID + F
GM = Q * F
FILLS = 2 * FULL + 1
GROUPS = [3, 3, 3, 3, 3, 1]
ZRING = 4
DENSE = 16
T1 = 512
T2 = 256


def field_pairs():
    return [(i, j) for i in range(F) for j in range(i, F)]


def build(nc, dense, ids, tables, W_top1, b_top1, W_top2, b_top2, W_top3, W1, W2,
          select_c, fold_c, ident_c, identf_c, y_out):
    with ExitStack() as ctx:
        def sb(name, shape, dt):
            return ctx.enter_context(nc.sbuf_tensor(name, shape, dt))

        def sem(name):
            return ctx.enter_context(nc.semaphore(name))

        ids_tile = [sb(f"ids_tile{u}", [P, F], I32) for u in range(2)]
        emb = [sb(f"emb{u}", [P, F * D], F32) for u in range(2)]
        gst = [sb(f"gst{u}", [P, PLACES, GS + 1], F32) for u in range(2)]
        resid = sb("resid", [P, PLACES, F], F32)
        parts = sb("parts", [P, PLACES, 3, F], BF16)
        xs = [sb(f"xs{u}", [3 * F, COLS], BF16) for u in range(2)]
        squares = sb("squares", [P, ZRING, COLS], F32)
        squares_rest = [sb(f"squares_rest{u}", [P, HALF * D], F32) for u in range(2)]
        xdiag = [sb(f"xdiag{u}", [P, HALF, GM], F32) for u in range(2)]
        arena = sb("arena", [P, 2 * FH * 2 * P], F32)
        gram2 = arena[:, 0:FH * 2 * P].rearrange("p (h b) -> p h b", h=FH)
        gram1 = arena[:, FH * 2 * P:2 * FH * 2 * P].rearrange("p (h b) -> p h b", h=FH)
        w_fin2 = sb("w_fin2", [P, FH, CONV2], F32)
        w_fin1 = sb("w_fin1", [P, FH, FIN1], F32)
        w_pairs = sb("w_pairs", [P, STEPS, HID], F32)
        w_rest = sb("w_rest", [P, Q, HID], F32)
        select = sb("select", [3 * F, FULL * P + 32], BF16)
        ident = sb("ident", [P, P], BF16)
        identf = sb("identf", [P, P], F32)
        fin_half = sb("fin_half", [FIN1, 2 * P], F32)
        z_conv2 = sb("z_conv2", [P, B], F32)
        z_rest = sb("z_rest", [FIN1 + DENSE, B], F32)
        dense_in = sb("dense_in", [P, TILES, DENSE], F32)
        wt1a = sb("wt1a", [CONV2, T1], F32)
        wt1b = sb("wt1b", [FIN1 + DENSE, T1], F32)
        wt2 = sb("wt2", [P, T1 // P, T2], F32)
        wt3 = sb("wt3", [P, T2 // P], F32)
        bias1 = sb("bias1", [P, T1 // P], F32)
        bias2 = sb("bias2", [P, T2 // P], F32)
        y_col = sb("y_col", [P, TILES], F32)
        y_row = sb("y_row", [TILES, P], F32)

        n_fold = W1T * STEPS * P // 2
        n_w1p = W1T * 3 * HID // 2
        fold = arena[:, 0:n_fold].bitcast(BF16).rearrange("p (t c) -> p t c", t=W1T)
        w1_parts = arena[:, n_fold:n_fold + n_w1p].bitcast(BF16).rearrange("p (s t k) -> p s t k", s=3, t=W1T)
        o = n_fold + n_w1p
        w1_in = arena[:, o:o + W1T * HID].rearrange("p (t k) -> p t k", t=W1T)
        w1_rem = arena[:, o + W1T * HID:o + 2 * W1T * HID].rearrange("p (t k) -> p t k", t=W1T)
        act1 = [arena[:, u * 2048:(u + 1) * 2048].rearrange("p (m b) -> p m b", m=T1 // P) for u in range(2)]
        act2 = [arena[:, 4096 + u * 1024:4096 + (u + 1) * 1024].rearrange("p (m b) -> p m b", m=T2 // P)
                for u in range(2)]

        sums = ctx.enter_context(nc.psum_tensor("sums", [P, 2, 1024], F32))
        hidden = ctx.enter_context(nc.psum_tensor("hidden", [P, 2, 512], F32))
        gram = ctx.enter_context(nc.psum_tensor("gram", [P, 512], F32))
        misc = ctx.enter_context(nc.psum_tensor("misc", [P, 512], F32))
        misc_bf = misc[:, :].bitcast(BF16)

        ids_loaded = [sem(f"ids_loaded{u}") for u in range(2)]
        tiles_begun = sem("tiles_begun")
        gathered = [sem(f"gathered{u}") for u in range(2)]
        consts_loaded = sem("consts_loaded")
        fold_loaded = sem("fold_loaded")
        w1_loaded = sem("w1_loaded")
        fin_loaded = sem("fin_loaded")
        mlp_loaded = sem("mlp_loaded")
        zeroed = sem("zeroed")
        w1_split = sem("w1_split")
        w_folded = sem("w_folded")
        w_ready = sem("w_ready")
        arena_zero = sem("arena_zero")
        dense_turned = sem("dense_turned")
        dense_ready = sem("dense_ready")
        xt_ready = sem("xt_ready")
        hi_ready = sem("hi_ready")
        resid_ready = sem("resid_ready")
        mid_ready = sem("mid_ready")
        parts_ready = sem("parts_ready")
        xs_turned = sem("xs_turned")
        xs_ready = sem("xs_ready")
        summed = sem("summed")
        squared = sem("squared")
        hid_first = sem("hid_first")
        hid_steps = sem("hid_steps")
        hid_turned = sem("hid_turned")
        xdiag_ready = sem("xdiag_ready")
        gram_filled = sem("gram_filled")
        gram2_out = sem("gram2_out")
        gram1_out = sem("gram1_out")
        fin_done = sem("fin_done")
        fin_half_out = sem("fin_half_out")
        fin_out = sem("fin_out")
        l1_done = sem("l1_done")
        l1_act = sem("l1_act")
        l1_act_v = sem("l1_act_v")
        l2_done = sem("l2_done")
        l2_act = sem("l2_act")
        y_done = sem("y_done")
        y_copied = sem("y_copied")
        stored = sem("stored")

        ids_t = ids.rearrange("(t p) f -> t p f", p=P)
        block = ctx.enter_context(nc.Block())

        @block.sync
        def _(sp):
            sp.dma_start(ids_tile[0][:, :], ids_t[0]).then_inc(ids_loaded[0], 16)
            sp.dma_start(ids_tile[1][:, :], ids_t[1]).then_inc(ids_loaded[1], 16)
            sp.wait_ge(zeroed, 1)
            w1_hid = W1[0:(W1T - 1) * P, 0:HID].rearrange("(t p) k -> p t k", p=P)
            sp.dma_start(w1_in[:, 0:W1T - 1, :], w1_hid).then_inc(w1_loaded, 16)
            sp.dma_start(w1_in[0:W1LAST, W1T - 1, :], W1[(W1T - 1) * P:F * F, 0:HID]).then_inc(w1_loaded, 16)
            sp.dma_start(fold, fold_c).then_inc(fold_loaded, 16)
            sp.dma_start(select[:, :], select_c).then_inc(consts_loaded, 16)
            sp.dma_start(ident[:, :], ident_c).then_inc(consts_loaded, 16)
            sp.dma_start(identf[:, :], identf_c).then_inc(consts_loaded, 16)
            sp.dma_start(dense_in[:, :, :], dense.rearrange("(t p) c -> p t c", p=P)).then_inc(consts_loaded, 16)
            sp.wait_ge(zeroed, 3)
            sp.dma_start(w_fin2[:, 0:FH - 1, :],
                         W2[0:(FH - 1) * P, :].rearrange("(h p) n -> p h n", p=P)).then_inc(fin_loaded, 16)
            sp.dma_start(w_fin2[0:HID, FH - 1, :], W2[(FH - 1) * P:F * HID, :]).then_inc(fin_loaded, 16)
            w1_fin = W1[:, HID:HID + FIN1].rearrange("(i r) k -> r i k", r=F)
            for h in range(FH):
                sp.dma_start(w_fin1[0:F, h, :], w1_fin[:, 2 * h, :]).then_inc(fin_loaded, 16)
                if h < FH - 1:
                    sp.dma_start(w_fin1[64:64 + F, h, :], w1_fin[:, 2 * h + 1, :]).then_inc(fin_loaded, 16)
            sp.dma_start(wt1a[:, :], W_top1[FIN1:FIN1 + CONV2, :]).then_inc(mlp_loaded, 16)
            sp.dma_start(wt1b[0:FIN1, :], W_top1[0:FIN1, :]).then_inc(mlp_loaded, 16)
            sp.dma_start(wt1b[FIN1:FIN1 + DENSE, :],
                         W_top1[FIN1 + CONV2:FIN1 + CONV2 + DENSE, :]).then_inc(mlp_loaded, 16)
            sp.dma_start(wt2[:, :, :], W_top2.rearrange("(m p) n -> p m n", p=P)).then_inc(mlp_loaded, 16)
            with nc.allow_non_contiguous_dma(reason="a few hundred words"):
                sp.dma_start(wt3[:, :], W_top3.rearrange("(m p) n -> p (m n)", p=P)).then_inc(mlp_loaded, 16)
                sp.dma_start(bias1[:, :], b_top1.rearrange("(m p) -> p m", p=P)).then_inc(mlp_loaded, 16)
                sp.dma_start(bias2[:, :], b_top2.rearrange("(m p) -> p m", p=P)).then_inc(mlp_loaded, 16)
            with sp.Fori(0, PAIRS - 1) as p:
                for u in range(2):
                    sp.wait_ge(gathered[u], 16 * F * (p + 1))
                    sp.dma_start(ids_tile[u][:, :], ids_t[bass.ds(2 * p + 2 + u, 1)].rearrange("o p f -> (o p) f")
                                 ).then_inc(ids_loaded[u], 16)
            sp.wait_ge(y_copied, 2)
            sp.dma_start(y_out.rearrange("(t p) c -> t (p c)", p=P), y_row[:, :]).then_inc(stored, 16)
            sp.wait_ge(stored, 16)

        @block.gpsimd
        def _(pool):
            def look_up(u):
                for f in range(F):
                    pool.indirect_dma_start(
                        out=emb[u][:, f * D:(f + 1) * D], out_offset=None, in_=tables[f],
                        in_offset=bass.IndirectOffsetOnAxis(ap=ids_tile[u][:, f:f + 1], axis=0),
                    ).then_inc(gathered[u], 16)

            for u in range(2):
                pool.wait_ge(ids_loaded[u], 16)
                look_up(u)
            with pool.Fori(0, PAIRS - 1) as p:
                for u in range(2):
                    pool.wait_ge(ids_loaded[u], 16 * (p + 2))
                    pool.wait_ge(xt_ready, 2 * p + u + 1)
                    pool.sem_inc(tiles_begun, 1)
                    look_up(u)

        @block.tensor
        def _(pe):
            def turn_parts(k, half, tile, chunk, after_final):
                pe.wait_ge(parts_ready, tile + 1)
                if after_final is not None:
                    pe.wait_ge(fin_out, after_final)
                if half or k or not isinstance(chunk, int) or chunk:
                    pe.wait_ge(xs_ready, 2 * chunk + half)
                for r in range(8):
                    place = (k % 2) * HALF + half * 8 + r
                    mm = nc.tensor.transpose(misc_bf[0:3 * F, r * P:(r + 1) * P],
                                             parts[:, place, :, :].rearrange("p s f -> p (s f)"), ident[:, :])
                mm.then_inc(xs_turned, 1)

            def sum_fields(k, t, chunk):
                for half in range(2 if t < FULL else 1):
                    fill = FILLS * chunk + 2 * t + half
                    slot = (FILLS * k + 2 * t + half) % 2
                    if not (isinstance(fill, int) and fill < 2):
                        pe.wait_ge(squared, fill - 1)
                    if t == 0:
                        pe.wait_ge(xs_ready, 2 * chunk + half + 1)
                    if t < FULL:
                        for n in range(2):
                            c0 = half * 1024 + n * 512
                            mm = nc.tensor.matmul(sums[:, slot, n * 512:(n + 1) * 512],
                                                  select[:, t * P:(t + 1) * P], xs[k % 2][:, c0:c0 + 512],
                                                  start=True, stop=True)
                    else:
                        x4 = xs[k % 2][:, :].rearrange("p (r q d) -> p r q d", q=Q, d=D)
                        for q in range(Q):
                            mm = nc.tensor.matmul(sums[32 * q:32 * q + 32, slot, 0:512],
                                                  select[:, FULL * P:FULL * P + 32], x4[:, :, q, :],
                                                  start=True, stop=True)
                    mm.then_inc(summed, 1)

            def hidden_step(k, t, chunk):
                pe.wait_ge(squared, FILLS * chunk + min(2 * t + 2, FILLS))
                for kb in range(2):
                    if t == 0 and not (isinstance(chunk, int) and chunk == 0):
                        pe.wait_ge(hid_turned, 2 * chunk - 1 + kb)
                    for q in range(Q):
                        if t < FULL:
                            w = w_pairs[:, t, kb * 32:(kb + 1) * 32]
                            z = squares[:, (FULL * k + t) % ZRING, :].rearrange("p (r q d) -> p r q d", q=Q, d=D)[
                                :, :, q, :]
                        else:
                            w = w_rest[:, q, kb * 32:(kb + 1) * 32]
                            z = squares_rest[k % 2][:, :]
                        mm = nc.tensor.matmul(hidden[32 * q:32 * q + 32, kb, :], w, z,
                                              start=(t == 0), stop=(t == STEPS - 1))
                    if t == STEPS - 1 and kb == 0:
                        mm.then_inc(hid_first, 1)
                mm.then_inc(hid_steps, 1)

            def gram_group(k, j, chunk):
                if j == 0:
                    pe.wait_ge(hid_turned, 2 * chunk + 2)
                    pe.wait_ge(xdiag_ready, chunk + 1)
                group = len(GROUPS) * chunk + j
                if not (isinstance(group, int) and group == 0):
                    pe.wait_ge(gram2_out, group)
                    pe.wait_ge(gram1_out, group)
                for r in range(GROUPS[j]):
                    place = sum(GROUPS[:j]) + r
                    mm = nc.tensor.matmul(gram[0:GS, r * GM:(r + 1) * GM],
                                          gst[k // 2][:, (k % 2) * HALF + place, 0:GS],
                                          xdiag[k % 2][:, place, :], start=True, stop=True)
                mm.then_inc(gram_filled, 1)

            def final_sums(pair):
                pe.wait_ge(gram2_out, 4 * len(GROUPS) * (pair + 1))
                for h in range(FH):
                    mm = nc.tensor.matmul(misc[:, 0:2 * P], w_fin2[:, h, :], gram2[:, h, :],
                                          start=(h == 0), stop=(h == FH - 1))
                pe.wait_ge(gram1_out, 4 * len(GROUPS) * (pair + 1))
                for h in range(FH):
                    c = h % 2
                    mm = nc.tensor.matmul(misc[64 * c:64 * c + 64, 2 * P:4 * P], w_fin1[0:64 + F, h, :],
                                          gram1[0:64 + F, h, :], start=(h < 2), stop=(h >= FH - 2))
                mm.then_inc(fin_done, 1)

            def pair_body(p, first, last):
                for k in range(4):
                    chunk = 4 * p + k
                    for t in range(STEPS):
                        kk, tt = (k, t + 2) if t + 2 < STEPS else (k + 1, t + 2 - STEPS)
                        if not (last and kk == 4):
                            sum_fields(kk, tt, 4 * p + kk)
                        hidden_step(k, t, chunk)
                        if t < len(GROUPS) and (k or not first):
                            gram_group((k - 1) % 4, t, chunk - 1)
                        if t in (2, 3) and not (last and k == 3):
                            turn_parts(k + 1, t - 2, 2 * p + (k + 1) // 2, chunk + 1,
                                       2 * p if k == 1 and t == 2 and not first else None)
                        if t == STEPS - 1 and k == 0 and not first:
                            final_sums(p - 1)

            pe.wait_ge(w1_split, 5)
            pe.wait_ge(fold_loaded, 16)
            for m in range(STEPS):
                for s in range(3):
                    for r in range(W1T):
                        mm = nc.tensor.matmul(gram[:, m * HID:(m + 1) * HID], fold[:, r, m * P:(m + 1) * P],
                                              w1_parts[:, s, r, :], start=(s == 0 and r == 0),
                                              stop=(s == 2 and r == W1T - 1))
            mm.then_inc(w_folded, 1)
            pe.wait_ge(consts_loaded, 64)
            for t in range(TILES):
                mm = nc.tensor.transpose(sums[0:DENSE, (t // 8), (t % 8) * P:(t % 8 + 1) * P],
                                         dense_in[:, t, :], identf[:, :])
            mm.then_inc(dense_turned, 1)
            turn_parts(0, 0, 0, 0, None)
            turn_parts(0, 1, 0, 0, None)
            pe.wait_ge(dense_ready, 1)
            sum_fields(0, 0, 0)
            sum_fields(0, 1, 0)
            pe.wait_ge(w_ready, 1)
            pair_body(0, True, False)
            pe.wait_ge(fin_loaded, 16 * (2 + F))
            with pe.Fori(1, PAIRS - 1) as p:
                pair_body(p, False, False)
            pair_body(PAIRS - 1, False, True)
            for j in range(len(GROUPS)):
                gram_group(3, j, 4 * PAIRS - 1)
            final_sums(PAIRS - 1)

            pe.wait_ge(mlp_loaded, 16 * 7)
            pe.wait_ge(fin_out, 2 * PAIRS)
            NB = B // 512

            def layer1(n):
                bs = slice(n * 512, (n + 1) * 512)
                for m in range(T1 // P):
                    i = n * (T1 // P) + m
                    if i >= 4:
                        pe.wait_ge(l1_act if i % 2 == 0 else l1_act_v, (i - 4) // 2 + 1)
                    o1 = sums[:, (i % 4) // 2, (i % 2) * 512:(i % 2 + 1) * 512]
                    nc.tensor.matmul(o1, wt1a[:, m * P:(m + 1) * P], z_conv2[:, bs], start=True, stop=False)
                    nc.tensor.matmul(o1, wt1b[:, m * P:(m + 1) * P], z_rest[:, bs], start=False,
                                     stop=True).then_inc(l1_done, 1)

            def layer2(n):
                pe.wait_ge(l1_act, 2 * n + 2)
                pe.wait_ge(l1_act_v, 2 * n + 2)
                for m in range(T2 // P):
                    if n:
                        pe.wait_ge(l2_act, 2 * (n - 1) + m + 1)
                    for c in range(T1 // P):
                        mm = nc.tensor.matmul(hidden[:, m, :], wt2[:, c, m * P:(m + 1) * P], act1[n % 2][:, c, :],
                                              start=(c == 0), stop=(c == T1 // P - 1))
                    mm.then_inc(l2_done, 1)

            def layer3(n):
                pe.wait_ge(l2_act, 2 * n + 2)
                for t in range(4):
                    for c in range(T2 // P):
                        mm = nc.tensor.matmul(gram[:, 4 * n + t:4 * n + t + 1], act2[n % 2][:, c, t * P:(t + 1) * P],
                                              wt3[:, c:c + 1], start=(c == 0), stop=(c == T2 // P - 1))
                mm.then_inc(y_done, 1)

            layer1(0)
            for n in range(NB):
                if n + 1 < NB:
                    layer1(n + 1)
                layer2(n)
                if n:
                    layer3(n - 1)
            layer3(NB - 1)
            pe.wait_ge(y_copied, 1)
            nc.tensor.transpose(misc[0:TILES, 0:P], y_col[:, :], identf[:, :]).then_inc(y_done, 1)

        @block.scalar
        def _(act):
            def leading_part(tile, u):
                act.wait_ge(xt_ready, tile + 1)
                if not (isinstance(tile, int) and tile == 0):
                    act.wait_ge(xs_turned, 4 * tile)
                nc.scalar.activation(parts[:, :, 0, :], gst[u][:, :, HID:GS], ACT.Copy).then_inc(hi_ready, 1)

            def middle_part(tile):
                act.wait_ge(resid_ready, tile + 1)
                nc.scalar.activation(parts[:, :, 1, :], resid[:, :, :], ACT.Copy).then_inc(mid_ready, 1)

            def square(k, t, chunk):
                for half in range(2 if t < FULL else 1):
                    fill = FILLS * chunk + 2 * t + half
                    slot = (FILLS * k + 2 * t + half) % 2
                    act.wait_ge(summed, fill + 1)
                    if t < FULL:
                        if half == 0 and not (isinstance(chunk, int) and FULL * chunk + t < ZRING):
                            back = STEPS * chunk + t - ZRING + 1 if t >= ZRING else (
                                STEPS * (chunk - 1) + t + FULL - ZRING + 1)
                            act.wait_ge(hid_steps, back)
                        nc.scalar.activation(squares[:, (FULL * k + t) % ZRING, half * 1024:(half + 1) * 1024],
                                             sums[:, slot, :], ACT.Square).then_inc(squared, 1)
                    else:
                        if not (isinstance(chunk, int) and chunk < 2):
                            act.wait_ge(hid_steps, STEPS * (chunk - 1))
                        nc.scalar.activation(squares_rest[k % 2][:, :], sums[:, slot, 0:512],
                                             ACT.Square).then_inc(squared, 1)

            def gram1_copy(k, j, chunk):
                act.wait_ge(gram_filled, len(GROUPS) * chunk + j + 1)
                if k == 0 and j == 0 and not (isinstance(chunk, int) and chunk == 0):
                    act.wait_ge(fin_done, pair_of(chunk))
                n = GROUPS[j] * Q
                col = k * HALF * Q + sum(GROUPS[:j]) * Q
                g = gram[HID:GS, 0:n * F].rearrange("p (b i) -> p b i", i=F)
                nc.scalar.activation(gram1[0:F, :, col:col + n].rearrange("p h b -> p b h"), g[:, :, 0::2],
                                     ACT.Copy)
                nc.scalar.activation(gram1[64:64 + F, 0:FH - 1, col:col + n].rearrange("p h b -> p b h"),
                                     g[:, :, 1::2], ACT.Copy).then_inc(gram1_out, 1)

            def fin_half_copy(pair):
                act.wait_ge(fin_done, pair + 1)
                nc.scalar.activation(fin_half[:, :], misc[64:128, 2 * P:4 * P], ACT.Copy).then_inc(fin_half_out, 1)

            pair_now = [0]

            def pair_of(chunk):
                return pair_now[0]

            def pair_body(p, first, last):
                pair_now[0] = p
                for k in range(4):
                    chunk = 4 * p + k
                    for t in range(STEPS):
                        kk, tt = (k, t + 2) if t + 2 < STEPS else (k + 1, t + 2 - STEPS)
                        if not (last and kk == 4):
                            square(kk, tt, 4 * p + kk)
                        if k % 2 and not (last and k == 3):
                            tile = 2 * p + (k + 1) // 2
                            if t == 0:
                                leading_part(tile, (k + 1) // 2 % 2)
                            if t == 1:
                                middle_part(tile)
                        if t < len(GROUPS) and (k or not first):
                            gram1_copy((k - 1) % 4, t, chunk - 1)
                        if t == STEPS - 1 and k == 0 and not first:
                            fin_half_copy(p - 1)

            leading_part(0, 0)
            middle_part(0)
            act.wait_ge(arena_zero, 2)
            square(0, 0, 0)
            square(0, 1, 0)
            pair_body(0, True, False)
            with act.Fori(1, PAIRS - 1) as p:
                pair_body(p, False, False)
            pair_body(PAIRS - 1, False, True)
            for j in range(len(GROUPS)):
                gram1_copy(3, j, 4 * PAIRS - 1)
            fin_half_copy(PAIRS - 1)
            act.wait_ge(mlp_loaded, 16 * 7)

            def relu1(n):
                if n >= 2:
                    act.wait_ge(l2_done, 2 * (n - 1))
                for m in range(0, T1 // P, 2):
                    i = n * (T1 // P) + m
                    act.wait_ge(l1_done, i + 1)
                    nc.scalar.activation(act1[n % 2][:, m, :], sums[:, (i % 4) // 2, 0:512], ACT.Relu,
                                         bias=bias1[:, m:m + 1]).then_inc(l1_act, 1)

            NB = B // 512
            relu1(0)
            for n in range(NB):
                if n + 1 < NB:
                    relu1(n + 1)
                for m in range(T2 // P):
                    act.wait_ge(l2_done, 2 * n + m + 1)
                    if n >= 2:
                        act.wait_ge(y_done, n - 1)
                    nc.scalar.activation(act2[n % 2][:, m, :], hidden[:, m, :], ACT.Relu,
                                         bias=bias2[:, m:m + 1]).then_inc(l2_act, 1)

        @block.vector
        def _(dve):
            pair_now = [0]

            def turn_x(tile, u, times):
                dve.wait_ge(gathered[u], 16 * F * times)
                if not (isinstance(tile, int) and tile < 2):
                    dve.wait_ge(gram_filled, 2 * len(GROUPS) * (tile - 1))
                nc.vector.transpose(gst[u][:, :, HID:GS].rearrange("p r f -> p f r"),
                                    emb[u][:, :].rearrange("p (f d) -> p f d", d=D)).then_inc(xt_ready, 1)

            def residual(tile, u):
                dve.wait_ge(hi_ready, tile + 1)
                if not (isinstance(tile, int) and tile == 0):
                    dve.wait_ge(parts_ready, tile)
                nc.vector.tensor_tensor(resid[:, :, :], gst[u][:, :, HID:GS], parts[:, :, 0, :],
                                        ALU.subtract).then_inc(resid_ready, 1)

            def last_part(tile):
                dve.wait_ge(mid_ready, tile + 1)
                nc.vector.tensor_tensor(parts[:, :, 2, :], resid[:, :, :], parts[:, :, 1, :],
                                        ALU.subtract).then_inc(parts_ready, 1)

            def copy_xs(k, half, chunk):
                dve.wait_ge(xs_turned, 2 * chunk + half + 1)
                if half == 0 and not (isinstance(chunk, int) and chunk < 2):
                    dve.wait_ge(summed, FILLS * (chunk - 1))
                nc.vector.tensor_copy(xs[k % 2][:, half * 1024:(half + 1) * 1024],
                                      misc_bf[0:3 * F, :]).then_inc(xs_ready, 1)

            def turn_hidden(k, chunk):
                for kb in range(2):
                    if kb == 0:
                        dve.wait_ge(hid_first, chunk + 1)
                        if not (isinstance(chunk, int) and chunk < 4):
                            dve.wait_ge(gram_filled, len(GROUPS) * (chunk - 3))
                    else:
                        dve.wait_ge(hid_steps, STEPS * (chunk + 1))
                    r0 = (k % 2) * HALF
                    nc.vector.transpose(gst[k // 2][:, r0:r0 + HALF, kb * 32:(kb + 1) * 32],
                                        hidden[:, kb, :].rearrange("p (r d) -> p r d", d=D)).then_inc(hid_turned, 1)

            def spread_x(k, chunk):
                if not (isinstance(chunk, int) and chunk < 2):
                    dve.wait_ge(gram_filled, len(GROUPS) * (chunk - 1))
                r0 = (k % 2) * HALF
                for q in range(Q):
                    rows = slice(32 * q, 32 * q + 32)
                    op = nc.vector.tensor_copy(xdiag[k % 2][rows, :, q * F:(q + 1) * F],
                                               gst[k // 2][rows, r0:r0 + HALF, HID:GS])
                op.then_inc(xdiag_ready, 1)

            def gram2_copy(k, j, chunk):
                dve.wait_ge(gram_filled, len(GROUPS) * chunk + j + 1)
                if k == 0 and j == 0 and not (isinstance(chunk, int) and chunk == 0):
                    dve.wait_ge(fin_done, pair_now[0])
                n = GROUPS[j] * Q
                col = k * HALF * Q + sum(GROUPS[:j]) * Q
                g = gram[0:HID, 0:n * F].rearrange("p (b i) -> p b i", i=F)
                nc.vector.tensor_copy(gram2[0:HID, :, col:col + n].rearrange("p h b -> p b h"), g[:, :, 0::2])
                nc.vector.tensor_copy(gram2[HID:P, 0:FH - 1, col:col + n].rearrange("p h b -> p b h"),
                                      g[:, :, 1::2]).then_inc(gram2_out, 1)

            def final_copy(pair):
                dve.wait_ge(fin_half_out, pair + 1)
                cols = bass.ds(pair * 2 * P, 2 * P)
                nc.vector.tensor_tensor(z_rest[0:FIN1, cols], misc[0:FIN1, 2 * P:4 * P], fin_half[:, :],
                                        ALU.add).then_inc(fin_out, 1)
                nc.vector.tensor_scalar(z_conv2[:, cols], misc[:, 0:2 * P], 1.0, None, ALU.mult).then_inc(fin_out, 1)

            def pair_body(p, first, last):
                pair_now[0] = p
                for k in range(4):
                    chunk = 4 * p + k
                    for t in range(STEPS):
                        if t == 0 and (k or not first):
                            turn_hidden((k - 1) % 4, chunk - 1)
                        if k % 2 and not (last and k == 3):
                            tile, u = 2 * p + (k + 1) // 2, (k + 1) // 2 % 2
                            if t == 0:
                                turn_x(tile, u, p + 1 + (k == 3))
                            if t == 1:
                                residual(tile, u)
                            if t == 2:
                                last_part(tile)
                        if t < len(GROUPS) and (k or not first):
                            gram2_copy((k - 1) % 4, t, chunk - 1)
                        if t in (2, 3) and not (last and k == 3):
                            copy_xs(k + 1, t - 2, chunk + 1)
                        if t == 4:
                            spread_x(k, chunk)
                        if t == STEPS - 1 and k == 0 and not first:
                            final_copy(p - 1)

            nc.vector.memset(w1_in[96:P, W1T - 1, :], 0.0).then_inc(zeroed, 1)
            nc.vector.memset(w_fin2[:, FH - 1, :], 0.0).then_inc(zeroed, 1)
            nc.vector.memset(w_fin1[:, :, :], 0.0).then_inc(zeroed, 1)
            nc.vector.memset(w_rest[:, :, :], 0.0).then_inc(zeroed, 1)
            for u in range(2):
                nc.vector.memset(xdiag[u][:, :, :], 0.0).then_inc(zeroed, 1)
            dve.wait_ge(w1_loaded, 32)
            nc.vector.tensor_copy(w1_parts[:, 0], w1_in).then_inc(w1_split, 1)
            dve.wait_ge(w1_split, 1)
            nc.vector.tensor_tensor(w1_rem, w1_in, w1_parts[:, 0], ALU.subtract).then_inc(w1_split, 1)
            dve.wait_ge(w1_split, 2)
            nc.vector.tensor_copy(w1_parts[:, 1], w1_rem).then_inc(w1_split, 1)
            dve.wait_ge(w1_split, 3)
            nc.vector.tensor_tensor(w1_in, w1_rem, w1_parts[:, 1], ALU.subtract).then_inc(w1_split, 1)
            dve.wait_ge(w1_split, 4)
            nc.vector.tensor_copy(w1_parts[:, 2], w1_in).then_inc(w1_split, 1)
            dve.wait_ge(w_folded, 1)
            dve.wait_ge(zeroed, 6)
            nc.vector.tensor_copy(w_pairs[:, :, :], gram[:, 0:STEPS * HID].rearrange("p (m k) -> p m k", k=HID))
            for q in range(Q):
                rows = slice(32 * q, 32 * q + 32)
                op = nc.vector.tensor_copy(w_rest[rows, q, :], gram[rows, FULL * HID:STEPS * HID])
            op.then_inc(w_ready, 1)
            dve.wait_ge(dense_turned, 1)
            for t in range(TILES):
                op = nc.vector.tensor_copy(
                    z_rest[FIN1:FIN1 + DENSE, t * P:(t + 1) * P].rearrange("p (r q) -> p q r", q=Q),
                    sums[0:DENSE, t // 8, (t % 8) * P:(t % 8 + 1) * P].rearrange("p (q r) -> p q r", q=Q))
            op.then_inc(dense_ready, 1)
            dve.wait_ge(w1_split, 5)
            nc.vector.memset(arena[:, 0:FH * 2 * P], 0.0).then_inc(arena_zero, 1)
            nc.vector.memset(arena[:, FH * 2 * P:2 * FH * 2 * P], 0.0).then_inc(arena_zero, 1)
            dve.wait_ge(arena_zero, 2)
            turn_x(0, 0, 1)
            residual(0, 0)
            last_part(0)
            copy_xs(0, 0, 0)
            copy_xs(0, 1, 0)
            pair_body(0, True, False)
            with dve.Fori(1, PAIRS - 1) as p:
                pair_body(p, False, False)
            pair_body(PAIRS - 1, False, True)
            turn_hidden(3, 4 * PAIRS - 1)
            for j in range(len(GROUPS)):
                gram2_copy(3, j, 4 * PAIRS - 1)
            final_copy(PAIRS - 1)
            dve.wait_ge(mlp_loaded, 16 * 7)
            for n in range(B // 512):
                if n >= 2:
                    dve.wait_ge(l2_done, 2 * (n - 1))
                for m in range(1, T1 // P, 2):
                    i = n * (T1 // P) + m
                    dve.wait_ge(l1_done, i + 1)
                    nc.vector.tensor_scalar(act1[n % 2][:, m, :], sums[:, (i % 4) // 2, 512:1024],
                                            bias1[:, m:m + 1], 0.0, ALU.add, ALU.max).then_inc(l1_act_v, 1)
            dve.wait_ge(y_done, B // 512)
            nc.vector.tensor_copy(y_col[:, :], gram[:, 0:TILES]).then_inc(y_copied, 1)
            dve.wait_ge(y_done, B // 512 + 1)
            nc.vector.tensor_copy(y_row[:, :].rearrange("t (q r) -> t q r", q=Q),
                                  misc[0:TILES, 0:P].rearrange("t (r q) -> t q r", q=Q)).then_inc(y_copied, 1)


def constants():
    import numpy as np

    pairs = field_pairs()
    select = np.zeros((3 * F, FULL * P + 32), "bfloat16")
    fold = np.zeros((W1T * P, STEPS * P), "bfloat16")
    for n, (i, j) in enumerate(pairs):
        for s in range(3):
            select[s * F + i, n] = 1
            select[s * F + j, n] = 1
        cols = [n] if n < FULL * P else [FULL * P + 32 * q + n - FULL * P for q in range(Q)]
        for c in cols:
            if i != j:
                fold[i * F + j, c] = fold[j * F + i, c] = 0.5
            else:
                fold[i * F + i, c] = 1
                for o in range(F):
                    if o != i:
                        fold[i * F + o, c] = fold[o * F + i, c] = -0.5
    fold = np.ascontiguousarray(fold.reshape(W1T, P, STEPS * P).transpose(1, 0, 2))
    return select, fold, np.eye(P, dtype="bfloat16"), np.eye(P, dtype="float32")


def kernel(**inputs):
    import numpy as np
    import concourse.bacc as bacc
    from concourse.bass_utils import run_bass_kernel_spmd

    nc = bacc.Bacc("TRN2", target_bir_lowering=False, num_devices=1)
    select, fold, ident, identf = constants()
    arrays = {n: np.ascontiguousarray(inputs[n]) for n in
              ["dense_ctx", "ids", *[f"tbl_{f}" for f in range(F)], "W_top1", "b_top1", "W_top2", "b_top2",
               "W_top3", "L0_rec_W1", "L0_rec_W2"]}
    arrays |= {"select": select, "fold": fold, "ident": ident, "identf": identf}
    arrays = {f"in_{n}": a for n, a in arrays.items()}
    d = {n: nc.dram_tensor(n, a.shape, mybir.dt.from_np(a.dtype), kind="ExternalInput").ap()
         for n, a in arrays.items()}
    y = nc.dram_tensor("out_y", (B, 1), F32, kind="ExternalOutput").ap()
    build(nc, d["in_dense_ctx"], d["in_ids"], [d[f"in_tbl_{f}"] for f in range(F)], d["in_W_top1"], d["in_b_top1"],
          d["in_W_top2"], d["in_b_top2"], d["in_W_top3"], d["in_L0_rec_W1"], d["in_L0_rec_W2"],
          d["in_select"], d["in_fold"], d["in_ident"], d["in_identf"], y)
    r = run_bass_kernel_spmd(nc, [arrays], core_ids=[0])
    return r.results[0]["out_y"]
```

```python
from contextlib import ExitStack

import concourse.bass as bass
from concourse import mybir

F32 = mybir.dt.float32
BF16 = mybir.dt.bfloat16
I32 = mybir.dt.int32
ALU = mybir.AluOpType
ACT = mybir.ActivationFunctionType

P = 128
F = 39
D = 32
Q = 4
HID = 64
FIN1 = 64
CONV2 = 128
B = 2048
TILES = B // P
PAIRS = TILES // 2
PLACES = 32
HALF = PLACES // 2
COLS = HALF * Q * D
THIRDS = 3
ROWS = THIRDS * F
PRODUCTS = [(0, 1), (1, 2), (1, 3), (0, 2), (2, 3), (0, 3)]
LAST_USE = {1: 3, 2: 5, 3: 6}
STEPS = len(PRODUCTS) + 1
LAST_AT = 64
LAST_SHIFT = LAST_AT % F
W1T = -(-F * F // P)
W1LAST = F * F - (W1T - 1) * P
FH = -(-F // 2)
GS = HID + F
GM = Q * F
GROUPS = [3, 3, 3, 3, 3, 1]
SPREAD = sum(GROUPS[:3])
ZRING = 3
AHEAD = 2
CRING = 4
DENSE = 16
T1 = 512
T2 = 256


ROTATION = [(0, 0, 0), (1, 4, 6), (3, 15, 14), (10, 20, 27)]
LEFT, = set(range(1, F // 2 + 1)) - {min((ROTATION[v][g] - ROTATION[u][g]) % F, (ROTATION[u][g] - ROTATION[v][g]) % F)
                                     for u, v in PRODUCTS for g in range(THIRDS)}


def build(nc, dense, ids, tables, W_top1, b_top1, W_top2, b_top2, W_top3, W1, W2,
          fold_c, identf_c, turning, y_out):
    with ExitStack() as ctx:
        def sb(name, shape, dt):
            return ctx.enter_context(nc.sbuf_tensor(name, shape, dt))

        def sem(name):
            return ctx.enter_context(nc.semaphore(name))

        ids_tile = [sb(f"ids_tile{u}", [P, F], I32) for u in range(2)]
        emb = [sb(f"emb{u}", [P, F * D], F32) for u in range(2)]
        gst = [sb(f"gst{u}", [P, PLACES, GS], F32) for u in range(2)]
        x_rows = [sb(f"x_rows{u}", [ROWS, COLS], F32) for u in range(2)]
        x_moved = [sb(f"x_moved{u}", [P, COLS], F32) for u in range(CRING)]
        blocks = sb("blocks", [P, ZRING, COLS], F32)
        last = sb("last", [LAST_AT + F, COLS], F32)
        xdiag = sb("xdiag", [P, HALF, GM], F32)
        arena = sb("arena", [P, 2 * FH * 2 * P], F32)
        gram2 = arena[:, 0:FH * 2 * P].rearrange("p (h b) -> p h b", h=FH)
        gram1 = arena[:, FH * 2 * P:2 * FH * 2 * P].rearrange("p (h b) -> p h b", h=FH)
        w_fin2 = sb("w_fin2", [P, FH, CONV2], F32)
        w_fin1 = sb("w_fin1", [P, FH, FIN1], F32)
        w_pairs = sb("w_pairs", [P, STEPS, HID], F32)
        identf = sb("identf", [P, P], F32)
        fin_half = sb("fin_half", [FIN1, P], F32)
        z_conv2 = sb("z_conv2", [P, B], F32)
        z_rest = sb("z_rest", [FIN1 + DENSE, B], F32)
        dense_in = sb("dense_in", [P, TILES, DENSE], F32)
        wt3 = sb("wt3", [P, T2 // P], F32)
        bias1 = sb("bias1", [P, T1 // P], F32)
        bias2 = sb("bias2", [P, T2 // P], F32)
        y_col = sb("y_col", [P, TILES], F32)
        y_row = sb("y_row", [TILES, P], F32)

        n_fold = W1T * STEPS * P // 2
        n_w1p = W1T * 3 * HID // 2
        fold = arena[:, 0:n_fold].bitcast(BF16).rearrange("p (t c) -> p t c", t=W1T)
        w1_parts = arena[:, n_fold:n_fold + n_w1p].bitcast(BF16).rearrange("p (s t k) -> p s t k", s=3, t=W1T)
        o = n_fold + n_w1p
        w1_in = arena[:, o:o + W1T * HID].rearrange("p (t k) -> p t k", t=W1T)
        w1_rem = arena[:, o + W1T * HID:o + 2 * W1T * HID].rearrange("p (t k) -> p t k", t=W1T)

        act1 = [blocks[:, u, :].rearrange("p (m b) -> p m b", m=T1 // P) for u in range(2)]
        act2 = [blocks[:, 2, u * 1024:(u + 1) * 1024].rearrange("p (m b) -> p m b", m=T2 // P) for u in range(2)]
        wt1a = x_moved[0][0:CONV2, 0:T1]
        wt1b = x_moved[0][0:FIN1 + DENSE, T1:2 * T1]
        wt2 = x_moved[0][:, 2 * T1:2 * T1 + T1 // P * T2].rearrange("p (m n) -> p m n", n=T2)
        hidden = ctx.enter_context(nc.psum_tensor("hidden", [P, 2, 2, 512], F32))
        gram = ctx.enter_context(nc.psum_tensor("gram", [P, 2, 512], F32))
        fin = ctx.enter_context(nc.psum_tensor("fin", [P, 512], F32))
        fin_conv2 = fin[:, 0:P]
        fin_final1 = fin[:, P:2 * P]
        misc = ctx.enter_context(nc.psum_tensor("misc", [P, 512], F32))

        ids_loaded = [sem(f"ids_loaded{u}") for u in range(2)]
        tiles_begun = sem("tiles_begun")
        moves_begun = sem("moves_begun")
        gathered = [sem(f"gathered{u}") for u in range(2)]
        consts_loaded = sem("consts_loaded")
        fold_loaded = sem("fold_loaded")
        w1_loaded = sem("w1_loaded")
        fin_loaded = sem("fin_loaded")
        mlp_loaded = sem("mlp_loaded")
        zeroed = sem("zeroed")
        w1_split = sem("w1_split")
        w_folded = sem("w_folded")
        w_ready = sem("w_ready")
        arena_zero = sem("arena_zero")
        dense_turned = sem("dense_turned")
        dense_ready = sem("dense_ready")
        xt_ready = sem("xt_ready")
        spilled = [sem(f"spilled{u}") for u in range(2)]
        turned = [sem(f"turned{u}") for u in range(2)]
        tripled = [sem(f"tripled{u}") for u in range(2)]
        moved = [sem(f"moved{u}") for u in range(CRING)]
        last_moved = sem("last_moved")
        multiplied = sem("multiplied")
        last_squared = sem("last_squared")
        hid_first = sem("hid_first")
        hid_steps = sem("hid_steps")
        hid_turned = sem("hid_turned")
        xdiag_ready = sem("xdiag_ready")
        gram_filled = sem("gram_filled")
        gram_out = sem("gram_out")
        fin_done = sem("fin_done")
        fin_half_out = sem("fin_half_out")
        fin_out = sem("fin_out")
        l1_done = sem("l1_done")
        l1_act = sem("l1_act")
        l1_act_v = sem("l1_act_v")
        l2_done = sem("l2_done")
        l2_act = sem("l2_act")
        y_done = sem("y_done")
        y_copied = sem("y_copied")
        stored = sem("stored")

        ids_t = ids.rearrange("(t p) f -> t p f", p=P)
        block = ctx.enter_context(nc.Block())

        def turns(k, p):
            return 16 * (2 * p + k // 2 + 1)

        @block.sync
        def _(sp):
            sp.dma_start(ids_tile[0][:, :], ids_t[0]).then_inc(ids_loaded[0], 16)
            sp.dma_start(ids_tile[1][:, :], ids_t[1]).then_inc(ids_loaded[1], 16)
            sp.wait_ge(zeroed, 1)
            w1_hid = W1[0:(W1T - 1) * P, 0:HID].rearrange("(t p) k -> p t k", p=P)
            sp.dma_start(w1_in[:, 0:W1T - 1, :], w1_hid).then_inc(w1_loaded, 16)
            sp.dma_start(w1_in[0:W1LAST, W1T - 1, :], W1[(W1T - 1) * P:F * F, 0:HID]).then_inc(w1_loaded, 16)
            sp.dma_start(fold, fold_c).then_inc(fold_loaded, 16)
            sp.dma_start(identf[:, :], identf_c).then_inc(consts_loaded, 16)
            sp.dma_start(dense_in[:, :, :], dense.rearrange("(t p) c -> p t c", p=P)).then_inc(consts_loaded, 16)
            sp.wait_ge(zeroed, 3)
            sp.dma_start(w_fin2[:, 0:FH - 1, :],
                         W2[0:(FH - 1) * P, :].rearrange("(h p) n -> p h n", p=P)).then_inc(fin_loaded, 16)
            sp.dma_start(w_fin2[0:HID, FH - 1, :], W2[(FH - 1) * P:F * HID, :]).then_inc(fin_loaded, 16)
            w1_fin = W1[:, HID:HID + FIN1].rearrange("(i r) k -> r i k", r=F)
            for h in range(FH):
                sp.dma_start(w_fin1[0:F, h, :], w1_fin[:, 2 * h, :]).then_inc(fin_loaded, 16)
                if h < FH - 1:
                    sp.dma_start(w_fin1[64:64 + F, h, :], w1_fin[:, 2 * h + 1, :]).then_inc(fin_loaded, 16)
            with nc.allow_non_contiguous_dma(reason="a few hundred words"):
                sp.dma_start(wt3[:, :], W_top3.rearrange("(m p) n -> p (m n)", p=P)).then_inc(mlp_loaded, 16)
                sp.dma_start(bias1[:, :], b_top1.rearrange("(m p) -> p m", p=P)).then_inc(mlp_loaded, 16)
                sp.dma_start(bias2[:, :], b_top2.rearrange("(m p) -> p m", p=P)).then_inc(mlp_loaded, 16)

            def spill(u, times, wait=True):
                sp.wait_ge(gathered[u], 16 * F * times)
                sp.sem_inc(moves_begun, 1)
                sp.dma_start(turning[u], emb[u][:, :]).then_inc(spilled[u], 16)

            def turn_rows(k, chunk, p):
                u = k // 2 % 2
                sp.wait_ge(spilled[u], 16 * (p + 1 + k // 4))
                if not (isinstance(chunk, int) and chunk < 2):
                    sp.wait_ge(multiplied, STEPS * (chunk - 1))
                    sp.wait_ge(last_squared, chunk - 1)
                    sp.sem_inc(moves_begun, 1)
                x_t = turning[u].rearrange("(s h) (f d) -> h f s d", h=2, d=D)
                sp.dma_start(x_rows[k % 2][0:F, :].rearrange("f (s d) -> f s d", d=D),
                             x_t[k % 2]).then_inc(turned[k % 2], 16)

            def move_copies(k, chunk, p):
                sp.wait_ge(turned[k % 2], turns(k, p))
                for g in range(1, THIRDS):
                    sp.dma_start(x_rows[k % 2][g * F:(g + 1) * F, :],
                                 x_rows[k % 2][0:F, :]).then_inc(tripled[k % 2], 16)
                sp.wait_ge(tripled[k % 2], 2 * turns(k, p))
                sp.sem_inc(moves_begun, 1)
                for u in range(1, 4):
                    slot = (3 * k + u - 1) % CRING
                    back = STEPS * (chunk - 2) + LAST_USE[3] if u == 1 else STEPS * (chunk - 1) + LAST_USE[u - 1]
                    if not (isinstance(back, int) and back <= 0):
                        sp.wait_ge(multiplied, back)
                        sp.sem_inc(moves_begun, 1)
                    for g in range(THIRDS):
                        r = ROTATION[u][g]
                        sp.dma_start(x_moved[slot][g * F:(g + 1) * F, :],
                                     x_rows[k % 2][r:r + F, :]).then_inc(moved[slot], 16)

            def move_last(k, chunk):
                if not (isinstance(chunk, int) and chunk == 0):
                    sp.wait_ge(hid_steps, STEPS * chunk)
                    sp.sem_inc(moves_begun, 1)
                r = (LAST_SHIFT + LEFT) % F
                sp.dma_start(last[LAST_AT:LAST_AT + F, :], x_rows[k % 2][r:r + F, :]).then_inc(last_moved, 16)

            def next_ids(u, p):
                sp.dma_start(ids_tile[u][:, :],
                             ids_t[bass.ds(2 * p + 2 + u, 1)].rearrange("o p f -> (o p) f")
                             ).then_inc(ids_loaded[u], 16)

            def pair_body(p, last_pair):
                for k in range(4):
                    chunk = 4 * p + k
                    move_last(k, chunk)
                    if not (last_pair and k == 3):
                        move_copies(k + 1, chunk + 1, p)
                    if k == 0:
                        if not last_pair:
                            next_ids(0, p)
                        spill(1, p + 1)
                        if not last_pair:
                            next_ids(1, p)
                    if k == 2 and not last_pair:
                        spill(0, p + 2)
                    if not (last_pair and k >= 2):
                        turn_rows(k + 2, chunk + 2, p)

            spill(0, 1)
            turn_rows(0, 0, 0)
            move_copies(0, 0, 0)
            turn_rows(1, 1, 0)
            sp.wait_ge(arena_zero, 4)
            pair_body(0, False)
            with sp.Fori(1, PAIRS - 1) as p:
                pair_body(p, False)
            pair_body(PAIRS - 1, True)
            sp.wait_ge(multiplied, STEPS * 4 * PAIRS)
            sp.dma_start(wt1a[:, :], W_top1[FIN1:FIN1 + CONV2, :]).then_inc(mlp_loaded, 16)
            sp.dma_start(wt1b[0:FIN1, :], W_top1[0:FIN1, :]).then_inc(mlp_loaded, 16)
            sp.dma_start(wt1b[FIN1:FIN1 + DENSE, :],
                         W_top1[FIN1 + CONV2:FIN1 + CONV2 + DENSE, :]).then_inc(mlp_loaded, 16)
            sp.dma_start(wt2[:, :, :], W_top2.rearrange("(m p) n -> p m n", p=P)).then_inc(mlp_loaded, 16)
            sp.wait_ge(y_copied, 2)
            sp.dma_start(y_out.rearrange("(t p) c -> t (p c)", p=P), y_row[:, :]).then_inc(stored, 16)
            sp.wait_ge(stored, 16)

        @block.gpsimd
        def _(pool):
            def look_up(u):
                for f in range(F):
                    pool.indirect_dma_start(
                        out=emb[u][:, f * D:(f + 1) * D], out_offset=None, in_=tables[f],
                        in_offset=bass.IndirectOffsetOnAxis(ap=ids_tile[u][:, f:f + 1], axis=0),
                    ).then_inc(gathered[u], 16)

            for u in range(2):
                pool.wait_ge(ids_loaded[u], 16)
                look_up(u)
            with pool.Fori(0, PAIRS - 1) as p:
                for u in range(2):
                    pool.wait_ge(ids_loaded[u], 16 * (p + 2))
                    pool.wait_ge(xt_ready, 2 * p + u + 1)
                    pool.wait_ge(spilled[u], 16 * (p + 1))
                    pool.sem_inc(tiles_begun, 1)
                    look_up(u)

        @block.tensor
        def _(pe):
            def hidden_step(k, t, chunk):
                pe.wait_ge(multiplied, STEPS * chunk + t + 1)
                if t == STEPS - 1:
                    pe.wait_ge(last_squared, chunk + 1)
                rows = ROWS if t < STEPS - 1 else LAST_AT + F
                block = blocks[0:ROWS, (6 * k + t) % ZRING, :] if t < STEPS - 1 else last[:, :]
                block = block.rearrange("p (q c) -> p q c", q=Q)
                for kb in range(2):
                    if t == 0 and not (isinstance(chunk, int) and chunk < 2):
                        pe.wait_ge(hid_turned, 2 * chunk - 3 + kb)
                    for q in range(Q):
                        mm = nc.tensor.matmul(hidden[32 * q:32 * q + 32, k % 2, kb, :],
                                              w_pairs[0:rows, t, kb * 32:(kb + 1) * 32], block[:, q, :],
                                              start=(t == 0), stop=(t == STEPS - 1))
                    if t == STEPS - 1 and kb == 0:
                        mm.then_inc(hid_first, 1)
                mm.then_inc(hid_steps, 1)

            def gram_group(k, j, chunk):
                if j == 0:
                    pe.wait_ge(hid_turned, 2 * chunk + 2)
                if j in (0, 3):
                    pe.wait_ge(xdiag_ready, 2 * chunk + 1 + j // 3)
                group = len(GROUPS) * chunk + j
                if not (isinstance(group, int) and group < 2):
                    pe.wait_ge(gram_out, group - 1)
                for r in range(GROUPS[j]):
                    place = sum(GROUPS[:j]) + r
                    mm = nc.tensor.matmul(gram[0:GS, j % 2, r * GM:(r + 1) * GM],
                                          gst[k // 2][:, 2 * place + k % 2, 0:GS],
                                          xdiag[:, place, :], start=True, stop=True)
                mm.then_inc(gram_filled, 1)

            def final_sums(t, parity, tile):
                if t == 0:
                    pe.wait_ge(gram_out, 2 * len(GROUPS) * (tile + 1))
                    if not (isinstance(tile, int) and tile == 0):
                        pe.wait_ge(fin_out, 2 * tile)
                cols = slice(parity * P, (parity + 1) * P)
                for n in range(2 * FH * t // STEPS, 2 * FH * (t + 1) // STEPS):
                    h = n % FH
                    if n < FH:
                        mm = nc.tensor.matmul(fin_conv2, w_fin2[:, h, :], gram2[:, h, cols],
                                              start=(h == 0), stop=(h == FH - 1))
                    else:
                        c = h % 2
                        mm = nc.tensor.matmul(fin_final1[64 * c:64 * c + 64, :], w_fin1[0:64 + F, h, :],
                                              gram1[0:64 + F, h, cols], start=(h < 2), stop=(h >= FH - 2))
                if t == STEPS - 1:
                    mm.then_inc(fin_done, 1)

            def pair_body(p, first):
                for k in range(4):
                    chunk = 4 * p + k
                    for t in range(STEPS):
                        hidden_step(k, t, chunk)
                        if t and (k or not first):
                            gram_group((k - 1) % 4, t - 1, chunk - 1)
                        if k == 1 and not first:
                            final_sums(t, 1, 2 * p - 1)
                        if k == 3:
                            if first and t == 0:
                                pe.wait_ge(fin_loaded, 16 * (2 + F))
                            final_sums(t, 0, 2 * p)

            pe.wait_ge(w1_split, 5)
            pe.wait_ge(fold_loaded, 16)
            for m in range(STEPS):
                for s in range(3):
                    for r in range(W1T):
                        mm = nc.tensor.matmul(misc[:, m * HID:(m + 1) * HID], fold[:, r, m * P:(m + 1) * P],
                                              w1_parts[:, s, r, :], start=(s == 0 and r == 0),
                                              stop=(s == 2 and r == W1T - 1))
            mm.then_inc(w_folded, 1)
            pe.wait_ge(consts_loaded, 32)
            for t in range(TILES):
                mm = nc.tensor.transpose(hidden[0:DENSE, t // 8, t // 4 % 2, (t % 4) * P:(t % 4 + 1) * P],
                                         dense_in[:, t, :], identf[:, :])
            mm.then_inc(dense_turned, 1)
            pe.wait_ge(dense_ready, 1)
            pe.wait_ge(w_ready, 1)
            pair_body(0, True)
            with pe.Fori(1, PAIRS) as p:
                pair_body(p, False)

            NB = B // 512

            def layer1(n, ms):
                bs = slice(n * 512, (n + 1) * 512)
                for m in ms:
                    i = n * (T1 // P) + m
                    if i >= 4:
                        pe.wait_ge(l1_act if i % 2 == 0 else l1_act_v, (i - 4) // 2 + 1)
                    o1 = hidden[:, (i % 4) // 2, i % 2, :]
                    nc.tensor.matmul(o1, wt1a[:, m * P:(m + 1) * P], z_conv2[:, bs], start=True, stop=False)
                    nc.tensor.matmul(o1, wt1b[:, m * P:(m + 1) * P], z_rest[:, bs], start=False,
                                     stop=True).then_inc(l1_done, 1)

            def layer2(n):
                pe.wait_ge(l1_act, 2 * n + 2)
                pe.wait_ge(l1_act_v, 2 * n + 2)
                for m in range(T2 // P):
                    if n:
                        pe.wait_ge(l2_act, 2 * (n - 1) + m + 1)
                    elif m == 0:
                        pe.wait_ge(gram_out, 4 * len(GROUPS) * PAIRS)
                    for c in range(T1 // P):
                        mm = nc.tensor.matmul(gram[:, m, :], wt2[:, c, m * P:(m + 1) * P], act1[n % 2][:, c, :],
                                              start=(c == 0), stop=(c == T1 // P - 1))
                    mm.then_inc(l2_done, 1)

            def layer3(n):
                pe.wait_ge(l2_act, 2 * n + 2)
                for t in range(4):
                    for c in range(T2 // P):
                        mm = nc.tensor.matmul(misc[:, 4 * n + t:4 * n + t + 1], act2[n % 2][:, c, t * P:(t + 1) * P],
                                              wt3[:, c:c + 1], start=(c == 0), stop=(c == T2 // P - 1))
                mm.then_inc(y_done, 1)

            for j in range(len(GROUPS)):
                gram_group(3, j, 4 * PAIRS - 1)
                if j == 1:
                    pe.wait_ge(mlp_loaded, 16 * 7)
                    pe.wait_ge(fin_out, 2 * (TILES - 1))
                if 1 <= j < T1 // P + 1:
                    layer1(0, [j - 1])
            for t in range(STEPS):
                final_sums(t, 1, TILES - 1)
            for n in range(NB):
                if n + 1 < NB:
                    if n == NB - 2:
                        pe.wait_ge(fin_out, 2 * TILES)
                    layer1(n + 1, range(T1 // P))
                layer2(n)
                if n:
                    layer3(n - 1)
            layer3(NB - 1)
            pe.wait_ge(y_copied, 1)
            nc.tensor.transpose(fin[0:TILES, 0:P], y_col[:, :], identf[:, :]).then_inc(y_done, 1)

        @block.scalar
        def _(act):
            def square_last(k, chunk, p):
                act.wait_ge(turned[k % 2], turns(k, p))
                if not (isinstance(chunk, int) and chunk == 0):
                    act.wait_ge(hid_steps, STEPS * chunk)
                nc.scalar.activation(last[0:F, :], x_rows[k % 2][0:F, :], ACT.Square).then_inc(last_squared, 1)

            def spread_x(k, part, chunk, tile):
                places = slice(0, SPREAD) if part == 0 else slice(SPREAD, HALF)
                if part == 0 and k % 2 == 0:
                    act.wait_ge(xt_ready, tile + 1)
                if not (isinstance(chunk, int) and chunk == 0):
                    act.wait_ge(gram_filled, len(GROUPS) * (chunk - 1) + 3 * (part + 1))
                for q in range(Q):
                    rows = slice(32 * q, 32 * q + 32)
                    op = nc.scalar.activation(
                        xdiag[rows, places, q * F:(q + 1) * F],
                        gst[k // 2][rows, 2 * places.start + k % 2:2 * places.stop:2, HID:GS], ACT.Copy)
                op.then_inc(xdiag_ready, 1)

            def gram_copy(k, j, chunk, tile):
                act.wait_ge(gram_filled, len(GROUPS) * chunk + j + 1)
                if k % 2 == 0 and j == 0 and not (isinstance(tile, int) and tile < 2):
                    act.wait_ge(fin_done, tile - 1)
                n = GROUPS[j] * Q
                col = k * HALF * Q + sum(GROUPS[:j]) * Q
                g = gram[:, j % 2, 0:n * F].rearrange("p (b i) -> p i b", i=F)
                nc.scalar.activation(gram2[0:HID, :, col:col + n], g[0:HID, 0::2, :], ACT.Copy)
                nc.scalar.activation(gram2[HID:P, 0:FH - 1, col:col + n], g[0:HID, 1::2, :], ACT.Copy)
                nc.scalar.activation(gram1[0:F, :, col:col + n], g[HID:GS, 0::2, :], ACT.Copy)
                nc.scalar.activation(gram1[64:64 + F, 0:FH - 1, col:col + n], g[HID:GS, 1::2, :],
                                     ACT.Copy).then_inc(gram_out, 1)

            def fin_half_copy(tile):
                act.wait_ge(fin_done, tile + 1)
                nc.scalar.activation(fin_half[:, :], fin_final1[64:128, :], ACT.Copy).then_inc(fin_half_out, 1)

            def pair_body(p, first):
                for k in range(4):
                    chunk = 4 * p + k
                    for t in range(STEPS):
                        if t == 0:
                            square_last(k, chunk, p)
                            if k == 0 and not first:
                                fin_half_copy(2 * p - 2)
                            if k == 2 and not first:
                                fin_half_copy(2 * p - 1)
                        elif k or not first:
                            gram_copy((k - 1) % 4, t - 1, chunk - 1, 2 * p + (k - 1) // 2)
                        if t in (4, 6):
                            spread_x(k, t // 2 - 2, chunk, 2 * p + k // 2)

            act.wait_ge(arena_zero, 4)
            pair_body(0, True)
            with act.Fori(1, PAIRS) as p:
                pair_body(p, False)
            fin_half_copy(TILES - 2)
            for j in range(len(GROUPS)):
                gram_copy(3, j, 4 * PAIRS - 1, TILES - 1)
            act.wait_ge(mlp_loaded, 16 * 7)

            def relu1(n):
                if n >= 2:
                    act.wait_ge(l2_done, 2 * (n - 1))
                for m in range(0, T1 // P, 2):
                    i = n * (T1 // P) + m
                    act.wait_ge(l1_done, i + 1)
                    nc.scalar.activation(act1[n % 2][:, m, :], hidden[:, (i % 4) // 2, 0, :], ACT.Relu,
                                         bias=bias1[:, m:m + 1]).then_inc(l1_act, 1)

            NB = B // 512
            relu1(0)
            fin_half_copy(TILES - 1)
            for n in range(NB):
                if n + 1 < NB:
                    relu1(n + 1)
                for m in range(T2 // P):
                    act.wait_ge(l2_done, 2 * n + m + 1)
                    if n >= 2:
                        act.wait_ge(y_done, n - 1)
                    nc.scalar.activation(act2[n % 2][:, m, :], gram[:, m, :], ACT.Relu,
                                         bias=bias2[:, m:m + 1]).then_inc(l2_act, 1)

        @block.vector
        def _(dve):
            def turn_x(tile, u, times):
                dve.wait_ge(gathered[u], 16 * F * times)
                if not (isinstance(tile, int) and tile < 2):
                    dve.wait_ge(gram_filled, 2 * len(GROUPS) * (tile - 1))
                nc.vector.transpose(gst[u][:, :, HID:GS].rearrange("p r f -> p f r"),
                                    emb[u][:, :].rearrange("p (f d) -> p f d", d=D)).then_inc(xt_ready, 1)

            def multiply(k, t, chunk, p):
                if t == STEPS - 1:
                    dve.wait_ge(last_moved, 16 * (chunk + 1))
                    rows = slice(LAST_AT, LAST_AT + F)
                    nc.vector.tensor_tensor(last[rows, :], x_rows[k % 2][rows, :], last[rows, :],
                                            ALU.mult).then_inc(multiplied, 1)
                    return
                if t < 3:
                    n = 3 * k + t
                    dve.wait_ge(moved[n % CRING], 16 * THIRDS * (3 * p + n // CRING + 1))
                if t == 0:
                    dve.wait_ge(tripled[k % 2], 2 * turns(k, p))
                if not (isinstance(chunk, int) and 6 * chunk + t < ZRING):
                    back = STEPS * chunk + t - ZRING + 1 if t >= ZRING else STEPS * (chunk - 1) + t + 6 - ZRING + 1
                    dve.wait_ge(hid_steps, back)

                def copy(u):
                    return x_moved[(3 * k + u - 1) % CRING][0:ROWS, :] if u else x_rows[k % 2][:, :]

                u, v = PRODUCTS[t]
                nc.vector.tensor_tensor(blocks[0:ROWS, (6 * k + t) % ZRING, :], copy(u), copy(v),
                                        ALU.mult).then_inc(multiplied, 1)

            def turn_hidden(k, chunk):
                for kb in range(2):
                    if kb == 0:
                        dve.wait_ge(hid_first, chunk + 1)
                        if not (isinstance(chunk, int) and chunk < 4):
                            dve.wait_ge(gram_filled, len(GROUPS) * (chunk - 3))
                    else:
                        dve.wait_ge(hid_steps, STEPS * (chunk + 1))
                    nc.vector.transpose(gst[k // 2][:, k % 2::2, kb * 32:(kb + 1) * 32],
                                        hidden[:, k % 2, kb, :].rearrange("p (r d) -> p r d", d=D)).then_inc(hid_turned, 1)

            def final_copy(tile):
                dve.wait_ge(fin_half_out, tile + 1)
                cols = bass.ds(tile * P, P)
                nc.vector.tensor_tensor(z_rest[0:FIN1, cols], fin_final1[0:FIN1, :], fin_half[:, :],
                                        ALU.add).then_inc(fin_out, 1)
                nc.vector.tensor_scalar(z_conv2[:, cols], fin_conv2, 1.0, None, ALU.mult).then_inc(fin_out, 1)

            def pair_body(p, first, last_pair):
                for k in range(4):
                    chunk = 4 * p + k
                    for t in range(STEPS):
                        if t == 0 and (k or not first):
                            turn_hidden((k - 1) % 4, chunk - 1)
                        kk, tt = (k, t + AHEAD) if t + AHEAD < STEPS else (k + 1, t + AHEAD - STEPS)
                        if not (last_pair and kk == 4):
                            multiply(kk, tt, 4 * p + kk, p)
                        if t == 0 and k % 2 == 0:
                            turn_x(2 * p + k // 2, k // 2, p + 1)
                        if t == 1 and k % 2 == 0 and not first:
                            final_copy(2 * p - 2 + k // 2)

            nc.vector.memset(w1_in[96:P, W1T - 1, :], 0.0).then_inc(zeroed, 1)
            nc.vector.memset(w_fin2[:, FH - 1, :], 0.0).then_inc(zeroed, 1)
            nc.vector.memset(w_fin1[:, :, :], 0.0).then_inc(zeroed, 1)
            nc.vector.memset(xdiag[:, :, :], 0.0).then_inc(arena_zero, 1)
            dve.wait_ge(w1_loaded, 32)
            nc.vector.tensor_copy(w1_parts[:, 0], w1_in).then_inc(w1_split, 1)
            dve.wait_ge(w1_split, 1)
            nc.vector.tensor_tensor(w1_rem, w1_in, w1_parts[:, 0], ALU.subtract).then_inc(w1_split, 1)
            dve.wait_ge(w1_split, 2)
            nc.vector.tensor_copy(w1_parts[:, 1], w1_rem).then_inc(w1_split, 1)
            dve.wait_ge(w1_split, 3)
            nc.vector.tensor_tensor(w1_in, w1_rem, w1_parts[:, 1], ALU.subtract).then_inc(w1_split, 1)
            dve.wait_ge(w1_split, 4)
            nc.vector.tensor_copy(w1_parts[:, 2], w1_in).then_inc(w1_split, 1)
            dve.wait_ge(w_folded, 1)
            nc.vector.tensor_copy(w_pairs[:, :, :], misc[:, 0:STEPS * HID].rearrange("p (m k) -> p m k", k=HID)
                                  ).then_inc(w_ready, 1)
            dve.wait_ge(dense_turned, 1)
            for t in range(TILES):
                op = nc.vector.tensor_copy(
                    z_rest[FIN1:FIN1 + DENSE, t * P:(t + 1) * P].rearrange("p (h r q) -> p q r h", h=2, q=Q),
                    hidden[0:DENSE, t // 8, t // 4 % 2, (t % 4) * P:(t % 4 + 1) * P].rearrange("p (q r h) -> p q r h", q=Q, h=2))
            op.then_inc(dense_ready, 1)
            dve.wait_ge(w1_split, 5)
            nc.vector.memset(arena[:, 0:FH * 2 * P], 0.0).then_inc(arena_zero, 1)
            nc.vector.memset(arena[:, FH * 2 * P:2 * FH * 2 * P], 0.0).then_inc(arena_zero, 1)
            nc.vector.memset(last[:, :], 0.0).then_inc(arena_zero, 1)
            for t in range(AHEAD):
                multiply(0, t, 0, 0)
            pair_body(0, True, False)
            with dve.Fori(1, PAIRS - 1) as p:
                pair_body(p, False, False)
            pair_body(PAIRS - 1, False, True)
            turn_hidden(3, 4 * PAIRS - 1)
            final_copy(TILES - 2)
            dve.wait_ge(mlp_loaded, 16 * 7)
            for n in range(B // 512):
                if n == 1:
                    final_copy(TILES - 1)
                if n >= 2:
                    dve.wait_ge(l2_done, 2 * (n - 1))
                for m in range(1, T1 // P, 2):
                    i = n * (T1 // P) + m
                    dve.wait_ge(l1_done, i + 1)
                    nc.vector.tensor_scalar(act1[n % 2][:, m, :], hidden[:, (i % 4) // 2, 1, :],
                                            bias1[:, m:m + 1], 0.0, ALU.add, ALU.max).then_inc(l1_act_v, 1)
            dve.wait_ge(y_done, B // 512)
            nc.vector.tensor_copy(y_col[:, :], misc[:, 0:TILES]).then_inc(y_copied, 1)
            dve.wait_ge(y_done, B // 512 + 1)
            nc.vector.tensor_copy(y_row[:, :].rearrange("t (q r h) -> t q r h", q=Q, h=2),
                                  fin[0:TILES, 0:P].rearrange("t (h r q) -> t q r h", h=2, q=Q)).then_inc(y_copied, 1)


def constants():
    import numpy as np

    fold = np.zeros((W1T * P, STEPS * P), "bfloat16")

    def pair(i, j, column):
        fold[i * F + j, column] = fold[j * F + i, column] = 1

    for t, (u, v) in enumerate(PRODUCTS):
        for g in range(THIRDS):
            for i in range(F):
                pair((i + ROTATION[u][g]) % F, (i + ROTATION[v][g]) % F, t * P + g * F + i)
    for i in range(F):
        pair(i, i, (STEPS - 1) * P + i)
        pair((LAST_SHIFT + i) % F, (LAST_SHIFT + i + LEFT) % F, (STEPS - 1) * P + LAST_AT + i)
    fold = np.ascontiguousarray(fold.reshape(W1T, P, STEPS * P).transpose(1, 0, 2))
    return fold, np.eye(P, dtype="float32")


def kernel(**inputs):
    import numpy as np
    import concourse.bacc as bacc
    from concourse.bass_utils import run_bass_kernel_spmd

    nc = bacc.Bacc("TRN2", target_bir_lowering=False, num_devices=1)
    fold, identf = constants()
    arrays = {n: np.ascontiguousarray(inputs[n]) for n in
              ["dense_ctx", "ids", *[f"tbl_{f}" for f in range(F)], "W_top1", "b_top1", "W_top2", "b_top2",
               "W_top3", "L0_rec_W1", "L0_rec_W2"]}
    arrays |= {"fold": fold, "identf": identf}
    arrays = {f"in_{n}": a for n, a in arrays.items()}
    d = {n: nc.dram_tensor(n, a.shape, mybir.dt.from_np(a.dtype), kind="ExternalInput").ap()
         for n, a in arrays.items()}
    y = nc.dram_tensor("out_y", (B, 1), F32, kind="ExternalOutput").ap()
    turning = nc.dram_tensor("turning", (2, P, F * D), F32, kind="Internal").ap()
    build(nc, d["in_dense_ctx"], d["in_ids"], [d[f"in_tbl_{f}"] for f in range(F)], d["in_W_top1"], d["in_b_top1"],
          d["in_W_top2"], d["in_b_top2"], d["in_W_top3"], d["in_L0_rec_W1"], d["in_L0_rec_W2"],
          d["in_fold"], d["in_identf"], turning, y)
    r = run_bass_kernel_spmd(nc, [arrays], core_ids=[0])
    return r.results[0]["out_y"]
```

```python
from contextlib import ExitStack

import concourse.bass as bass
from concourse import mybir

F32 = mybir.dt.float32
BF16 = mybir.dt.bfloat16
I32 = mybir.dt.int32
ALU = mybir.AluOpType
ACT = mybir.ActivationFunctionType

P = 128
F = 39
D = 32
Q = 4
HID = 64
HALF_HID = HID // 2
FIN1 = 64
CONV2 = 128
B = 2048
TILES = B // P
PAIRS = TILES // 2
PLACES = 32
HALF = PLACES // 2
COLS = HALF * Q * D
THIRDS = 3
ROWS = THIRDS * F
PRODUCTS = [(0, 1), (1, 2), (1, 3), (0, 2), (2, 3), (0, 3)]
LAST_USE = {1: 3, 2: 5, 3: 6}
STEPS = len(PRODUCTS) + 1
LAST_AT = 64
LAST_SHIFT = LAST_AT % F
W1T = -(-F * F // P)
W1LAST = F * F - (W1T - 1) * P
FH = -(-F // 2)
SLOT = 32
TOP = F - SLOT
F1A = -(-F // 4)
F1B = -(-TOP // 4)
F1 = F1A + F1B
GS = HID + F
GM = Q * F
GROUPS = [3, 3, 2]
SPREAD = 2 * sum(GROUPS[:2])
ZRING = 4
AHEAD = 3
CRING = 4
DENSE = 16
PARTS = [slice(0, 2 * F // 3), slice(2 * F // 3, F)]
T1 = 512
T2 = 256


ROTATION = [(0, 0, 0), (1, 4, 6), (3, 15, 14), (10, 20, 27)]
LEFT, = set(range(1, F // 2 + 1)) - {min((ROTATION[v][g] - ROTATION[u][g]) % F, (ROTATION[u][g] - ROTATION[v][g]) % F)
                                     for u, v in PRODUCTS for g in range(THIRDS)}


def build(nc, dense, ids, tables, W_top1, b_top1, W_top2, b_top2, W_top3, W1, W2,
          fold_c, identf_c, turning, y_out):
    with ExitStack() as ctx:
        def sb(name, shape, dt):
            return ctx.enter_context(nc.sbuf_tensor(name, shape, dt))

        def sem(name):
            return ctx.enter_context(nc.semaphore(name))

        ids_tile = [sb(f"ids_tile{u}", [P, F], I32) for u in range(2)]
        emb = [sb(f"emb{u}", [P, F * D], F32) for u in range(2)]
        gst = [sb(f"gst{u}", [P, PLACES, GS], F32) for u in range(2)]
        x_rows = [sb(f"x_rows{u}", [ROWS, COLS], F32) for u in range(2)]
        x_moved = [sb(f"x_moved{u}", [P, COLS], F32) for u in range(CRING)]
        blocks = sb("blocks", [P, ZRING, COLS], F32)
        last = sb("last", [LAST_AT + F, COLS], F32)
        xdiag = sb("xdiag", [P, HALF, GM], F32)
        arena = sb("arena", [P, (FH + F1) * 2 * P], F32)
        gram2 = arena[:, 0:FH * 2 * P].rearrange("p (h b) -> p h b", h=FH)
        gram1 = arena[:, FH * 2 * P:].rearrange("p (h b) -> p h b", h=F1)
        w_fin2 = sb("w_fin2", [P, FH, CONV2], F32)
        w_fin1 = sb("w_fin1", [P, F1, FIN1], F32)
        w_swapped = sb("w_swapped", [P, F1B, FIN1], F32)
        w_pairs = sb("w_pairs", [P, STEPS, HID + HALF_HID], F32)
        hid_high = sb("hid_high", [P, 512], F32)
        identf = sb("identf", [P, P], F32)
        fin_half = sb("fin_half", [FIN1, P], F32)
        z_conv2 = sb("z_conv2", [P, P], F32)
        z_rest = sb("z_rest", [FIN1 + DENSE, P], F32)
        dense_rows = sb("dense_rows", [FIN1 + DENSE, B], F32)
        wt1a = sb("wt1a", [CONV2, T1], F32)
        wt1b = sb("wt1b", [FIN1 + DENSE, T1], F32)
        wt2 = sb("wt2", [P, T1 // P, T2], F32)
        act1 = sb("act1", [P, T1 // P, P], F32)
        act2 = sb("act2", [P, T2 // P, P], F32)
        dense_in = sb("dense_in", [P, TILES, DENSE], F32)
        wt3 = sb("wt3", [P, T2 // P], F32)
        bias1 = sb("bias1", [P, T1 // P], F32)
        bias2 = sb("bias2", [P, T2 // P], F32)
        y_col = sb("y_col", [P, TILES], F32)
        y_row = sb("y_row", [TILES, P], F32)

        n_fold = W1T * STEPS * P // 2
        n_w1p = W1T * 3 * HID // 2
        fold = arena[:, 0:n_fold].bitcast(BF16).rearrange("p (t c) -> p t c", t=W1T)
        w1_parts = arena[:, n_fold:n_fold + n_w1p].bitcast(BF16).rearrange("p (s t k) -> p s t k", s=3, t=W1T)
        o = n_fold + n_w1p
        w1_in = arena[:, o:o + W1T * HID].rearrange("p (t k) -> p t k", t=W1T)
        w1_rem = arena[:, o + W1T * HID:o + 2 * W1T * HID].rearrange("p (t k) -> p t k", t=W1T)

        hidden = ctx.enter_context(nc.psum_tensor("hidden", [P, 2, 2, 512], F32))
        gram = ctx.enter_context(nc.psum_tensor("gram", [P, 2, 512], F32))
        fin = ctx.enter_context(nc.psum_tensor("fin", [P, 512], F32))
        fin_conv2 = fin[:, 0:P]
        fin_final1 = fin[:, P:2 * P]
        outs2 = fin[:, 2 * P:4 * P].rearrange("p (m b) -> p m b", m=T2 // P)
        spare = ctx.enter_context(nc.psum_tensor("spare", [P, 512], F32))
        outs1 = spare[:, :].rearrange("p (m b) -> p m b", m=T1 // P)

        ids_loaded = [sem(f"ids_loaded{u}") for u in range(2)]
        tiles_begun = sem("tiles_begun")
        moves_begun = sem("moves_begun")
        gathered = [[sem(f"gathered{u}_{s}") for s in range(2)] for u in range(2)]
        consts_loaded = sem("consts_loaded")
        fold_loaded = sem("fold_loaded")
        w1_loaded = sem("w1_loaded")
        fin_loaded = sem("fin_loaded")
        fin_weights = sem("fin_weights")
        mlp_loaded = sem("mlp_loaded")
        zeroed = sem("zeroed")
        w1_split = sem("w1_split")
        w_folded = sem("w_folded")
        w_ready = sem("w_ready")
        cleared = sem("cleared")
        dense_turned = sem("dense_turned")
        dense_ready = sem("dense_ready")
        xt_ready = sem("xt_ready")
        spilled = [[sem(f"spilled{u}_{s}") for s in range(2)] for u in range(2)]
        turned = [sem(f"turned{u}") for u in range(2)]
        tripled = [sem(f"tripled{u}") for u in range(2)]
        moved = [sem(f"moved{u}") for u in range(CRING)]
        last_moved = sem("last_moved")
        multiplied = sem("multiplied")
        last_squared = sem("last_squared")
        hid_first = sem("hid_first")
        hid_steps = sem("hid_steps")
        hid_sorted = sem("hid_sorted")
        hid_turned = sem("hid_turned")
        xdiag_ready = sem("xdiag_ready")
        gram_filled = sem("gram_filled")
        gram_out = sem("gram_out")
        fin_done = sem("fin_done")
        fin_half_out = sem("fin_half_out")
        fin_out = sem("fin_out")
        l1_done = sem("l1_done")
        l1_act = sem("l1_act")
        l2_done = sem("l2_done")
        l2_act = sem("l2_act")
        y_done = sem("y_done")
        y_copied = sem("y_copied")
        y_turned = sem("y_turned")
        y_ready = sem("y_ready")
        stored = sem("stored")

        ids_t = ids.rearrange("(t p) f -> t p f", p=P)
        block = ctx.enter_context(nc.Block())

        def turns(k, p):
            return 2 * 16 * (2 * p + k // 2 + 1)

        def triples(k, p):
            if k % 2:
                return turns(k, p)
            return turns(k, p) + 2 * 16 * (1 if k == 0 and isinstance(p, int) and p == 0 else 2)

        def gathered_all(engine, u, times):
            for s, part in enumerate(PARTS):
                engine.wait_ge(gathered[u][s], 16 * (part.stop - part.start) * times)

        @block.sync
        def _(sp):
            sp.dma_start(ids_tile[0][:, :], ids_t[0]).then_inc(ids_loaded[0], 16)
            sp.dma_start(ids_tile[1][:, :], ids_t[1]).then_inc(ids_loaded[1], 16)
            sp.wait_ge(zeroed, 1)
            w1_hid = W1[0:(W1T - 1) * P, 0:HID].rearrange("(t p) k -> p t k", p=P)
            sp.dma_start(w1_in[:, 0:W1T - 1, :], w1_hid).then_inc(w1_loaded, 16)
            sp.dma_start(w1_in[0:W1LAST, W1T - 1, :], W1[(W1T - 1) * P:F * F, 0:HID]).then_inc(w1_loaded, 16)
            sp.dma_start(fold, fold_c).then_inc(fold_loaded, 16)
            sp.dma_start(identf[:, :], identf_c).then_inc(consts_loaded, 16)
            sp.dma_start(dense_in[:, :, :], dense.rearrange("(t p) c -> p t c", p=P)).then_inc(consts_loaded, 16)
            sp.wait_ge(zeroed, 4)
            sp.dma_start(w_fin2[:, 0:FH - 1, :],
                         W2[0:(FH - 1) * P, :].rearrange("(h p) n -> p h n", p=P)).then_inc(fin_loaded, 16)
            sp.dma_start(w_fin2[0:HID, FH - 1, :], W2[(FH - 1) * P:F * HID, :]).then_inc(fin_loaded, 16)
            w1_fin = W1[:, HID:HID + FIN1].rearrange("(i j) k -> j i k", j=F)
            for c in range(4):
                rows = slice(c * SLOT, (c + 1) * SLOT)
                top = slice(c * SLOT, c * SLOT + TOP)
                n = len(range(c, F, 4))
                n_top = len(range(c, TOP, 4))
                sp.dma_start(w_fin1[rows, 0:n, :], w1_fin[0:SLOT, c::4, :]).then_inc(fin_loaded, 16)
                sp.dma_start(w_fin1[top, F1A:F1A + n_top, :],
                             w1_fin[SLOT:F, SLOT + c::4, :]).then_inc(fin_loaded, 16)
                sp.dma_start(w_swapped[rows, 0:n_top, :],
                             w1_fin[SLOT + c::4, 0:SLOT, :].rearrange("i j k -> j i k")).then_inc(fin_loaded, 16)
            with nc.allow_non_contiguous_dma(reason="a few hundred words"):
                sp.dma_start(wt3[:, :], W_top3.rearrange("(m p) n -> p (m n)", p=P)).then_inc(mlp_loaded, 16)
                sp.dma_start(bias1[:, :], b_top1.rearrange("(m p) -> p m", p=P)).then_inc(mlp_loaded, 16)
                sp.dma_start(bias2[:, :], b_top2.rearrange("(m p) -> p m", p=P)).then_inc(mlp_loaded, 16)
            sp.dma_start(wt1a[:, :], W_top1[FIN1:FIN1 + CONV2, :]).then_inc(mlp_loaded, 16)
            sp.dma_start(wt1b[0:FIN1, :], W_top1[0:FIN1, :]).then_inc(mlp_loaded, 16)
            sp.dma_start(wt1b[FIN1:FIN1 + DENSE, :],
                         W_top1[FIN1 + CONV2:FIN1 + CONV2 + DENSE, :]).then_inc(mlp_loaded, 16)
            sp.dma_start(wt2[:, :, :], W_top2.rearrange("(m p) n -> p m n", p=P)).then_inc(mlp_loaded, 16)

            def spill_and_turn(u, times, k, chunk, p, thrice):
                x_t = turning[k // 2 % 2].rearrange("(s h) (f d) -> h f s d", h=2, d=D)
                for s, part in enumerate(PARTS):
                    cols = slice(part.start * D, part.stop * D)
                    if k % 2 == 0:
                        sp.wait_ge(gathered[u][s], 16 * (part.stop - part.start) * times)
                        sp.sem_inc(moves_begun, 1)
                        sp.dma_start(turning[u][:, cols], emb[u][:, cols]).then_inc(spilled[u][s], 16)
                        sp.wait_ge(spilled[u][s], 16 * times)
                    if s == 0 and not (isinstance(chunk, int) and chunk < 2):
                        sp.wait_ge(multiplied, STEPS * (chunk - 1))
                        sp.wait_ge(last_squared, chunk - 1)
                    sp.sem_inc(moves_begun, 1)
                    for g in range(THIRDS if thrice else 1):
                        sp.dma_start(x_rows[k % 2][g * F + part.start:g * F + part.stop, :].rearrange(
                            "f (s d) -> f s d", d=D), x_t[k % 2, part]).then_inc((tripled if g else turned)[k % 2], 16)

            def move_copies(k, chunk, p, thrice=False):
                sp.wait_ge(turned[k % 2], turns(k, p))
                for g in range(THIRDS if thrice else 1, THIRDS):
                    sp.dma_start(x_rows[k % 2][g * F:(g + 1) * F, :],
                                 x_rows[k % 2][0:F, :]).then_inc(tripled[k % 2], 16)
                sp.wait_ge(tripled[k % 2], triples(k, p))
                sp.sem_inc(moves_begun, 1)
                for u in range(1, 4):
                    slot = (3 * k + u - 1) % CRING
                    back = STEPS * (chunk - 2) + LAST_USE[3] if u == 1 else STEPS * (chunk - 1) + LAST_USE[u - 1]
                    if not (isinstance(back, int) and back <= 0):
                        sp.wait_ge(multiplied, back)
                        sp.sem_inc(moves_begun, 1)
                    for g in range(THIRDS):
                        r = ROTATION[u][g]
                        sp.dma_start(x_moved[slot][g * F:(g + 1) * F, :],
                                     x_rows[k % 2][r:r + F, :]).then_inc(moved[slot], 16)

            def move_last(k, chunk):
                if not (isinstance(chunk, int) and chunk == 0):
                    sp.wait_ge(hid_steps, STEPS * chunk)
                    sp.sem_inc(moves_begun, 1)
                r = (LAST_SHIFT + LEFT) % F
                sp.dma_start(last[LAST_AT:LAST_AT + F, :], x_rows[k % 2][r:r + F, :]).then_inc(last_moved, 16)

            def next_ids(u, p):
                sp.dma_start(ids_tile[u][:, :],
                             ids_t[bass.ds(2 * p + 2 + u, 1)].rearrange("o p f -> (o p) f")
                             ).then_inc(ids_loaded[u], 16)

            def pair_body(p, first, last_pair):
                for k in range(4):
                    chunk = 4 * p + k
                    move_last(k, chunk)
                    if not (last_pair and k == 3):
                        move_copies(k + 1, chunk + 1, p, first and k == 1)
                    if k == 0 and not last_pair:
                        next_ids(0, p)
                    if not (last_pair and k >= 2):
                        spill_and_turn((k + 2) // 2 % 2, p + 1 + k // 2, k + 2, chunk + 2, p, first and k == 0)
                    if k == 0 and not last_pair:
                        next_ids(1, p)

            spill_and_turn(0, 1, 0, 0, 0, True)
            move_copies(0, 0, 0, True)
            spill_and_turn(0, 1, 1, 1, 0, False)
            sp.wait_ge(cleared, 4)
            pair_body(0, True, False)
            with sp.Fori(1, PAIRS - 1) as p:
                pair_body(p, False, False)
            pair_body(PAIRS - 1, False, True)
            sp.wait_ge(y_ready, 1)
            sp.dma_start(y_out.rearrange("(t p) c -> t (p c)", p=P), y_row[:, :]).then_inc(stored, 16)
            sp.wait_ge(stored, 16)

        @block.gpsimd
        def _(pool):
            def look_up(u):
                for f in range(F):
                    pool.indirect_dma_start(
                        out=emb[u][:, f * D:(f + 1) * D], out_offset=None, in_=tables[f],
                        in_offset=bass.IndirectOffsetOnAxis(ap=ids_tile[u][:, f:f + 1], axis=0),
                    ).then_inc(gathered[u][f >= PARTS[1].start], 16)

            for u in range(2):
                pool.wait_ge(ids_loaded[u], 16)
                look_up(u)
            with pool.Fori(0, PAIRS - 1) as p:
                for u in range(2):
                    pool.wait_ge(ids_loaded[u], 16 * (p + 2))
                    pool.wait_ge(xt_ready, 2 * p + u + 1)
                    for s in range(2):
                        pool.wait_ge(spilled[u][s], 16 * (p + 1))
                    pool.sem_inc(tiles_begun, 1)
                    look_up(u)

        @block.tensor
        def _(pe):
            def hidden_step(k, t, chunk):
                pe.wait_ge(multiplied, STEPS * chunk + t + 1)
                if t == STEPS - 1:
                    pe.wait_ge(last_squared, chunk + 1)
                rows = ROWS if t < STEPS - 1 else LAST_AT + F
                block = blocks[0:ROWS, (6 * k + t) % ZRING, :] if t < STEPS - 1 else last[:, :]
                block = block.rearrange("p (q c) -> p q c", q=Q)
                if t == 0 and not (isinstance(chunk, int) and chunk < 2):
                    pe.wait_ge(hid_turned, 2 * chunk - 2)
                for bank in range(2):
                    for c in range(2):
                        mm = nc.tensor.matmul(hidden[64 * c:64 * c + 64, k % 2, bank, :],
                                              w_pairs[0:rows, t, bank * HALF_HID:bank * HALF_HID + HID],
                                              block[:, 2 * c + bank, :], start=(t == 0), stop=(t == STEPS - 1))
                    if t == STEPS - 1 and bank == 0:
                        mm.then_inc(hid_first, 1)
                mm.then_inc(hid_steps, 1)

            def gram_group(k, j, chunk):
                if j == 0:
                    pe.wait_ge(hid_turned, 2 * chunk + 2)
                if j in (0, 2):
                    pe.wait_ge(xdiag_ready, 2 * chunk + 1 + j // 2)
                group = len(GROUPS) * chunk + j
                if not (isinstance(group, int) and group == 0):
                    pe.wait_ge(gram_out, group)
                for bank in range(2):
                    for r in range(GROUPS[j]):
                        place = 2 * sum(GROUPS[:j]) + bank * GROUPS[j] + r
                        mm = nc.tensor.matmul(gram[0:GS, bank, r * GM:(r + 1) * GM],
                                              gst[k // 2][:, 2 * place + k % 2, 0:GS],
                                              xdiag[:, place, :], start=True, stop=True)
                mm.then_inc(gram_filled, 1)

            def final_sums(j, parity, tile):
                if j == 0:
                    pe.wait_ge(gram_out, 2 * len(GROUPS) * (tile + 1))
                    if not (isinstance(tile, int) and tile == 0):
                        pe.wait_ge(fin_out, 3 * tile)
                        pe.wait_ge(l2_act, tile)
                cols = slice(parity * P, (parity + 1) * P)
                n_all = FH + F1
                for n in range(n_all * j // 3, n_all * (j + 1) // 3):
                    if n < FH:
                        mm = nc.tensor.matmul(fin_conv2, w_fin2[:, n, :], gram2[:, n, cols],
                                              start=(n == 0), stop=(n == FH - 1))
                    else:
                        h = n - FH
                        c = h % 2
                        mm = nc.tensor.matmul(fin_final1[64 * c:64 * c + 64, :], w_fin1[:, h, :],
                                              gram1[:, h, cols], start=(h < 2), stop=(h >= F1 - 2))
                if j == 2:
                    mm.then_inc(fin_done, 1)

            def layer1(tile):
                pe.wait_ge(fin_out, 3 * (tile + 1))
                if not (isinstance(tile, int) and tile == 0):
                    pe.wait_ge(y_copied, tile)
                for m in range(T1 // P):
                    nc.tensor.matmul(outs1[:, m, :], wt1a[:, m * P:(m + 1) * P], z_conv2[:, :], start=True, stop=False)
                    mm = nc.tensor.matmul(outs1[:, m, :], wt1b[:, m * P:(m + 1) * P], z_rest[:, :],
                                          start=False, stop=True)
                mm.then_inc(l1_done, 1)

            def layer2(tile):
                pe.wait_ge(l1_act, tile + 1)
                for m in range(T2 // P):
                    for c in range(T1 // P):
                        mm = nc.tensor.matmul(outs2[:, m, :], wt2[:, c, m * P:(m + 1) * P], act1[:, c, :],
                                              start=(c == 0), stop=(c == T1 // P - 1))
                mm.then_inc(l2_done, 1)

            def layer3(tile):
                pe.wait_ge(l2_act, tile + 1)
                for c in range(T2 // P):
                    mm = nc.tensor.matmul(spare[:, 0:1], act2[:, c, :], wt3[:, c:c + 1],
                                          start=(c == 0), stop=(c == T2 // P - 1))
                mm.then_inc(y_done, 1)

            def pair_body(p, first):
                for k in range(4):
                    chunk = 4 * p + k
                    for t in range(STEPS):
                        hidden_step(k, t, chunk)
                        if t in (2, 4, 6):
                            j = t // 2 - 1
                            if k or not first:
                                gram_group((k - 1) % 4, j, chunk - 1)
                            if k == 1 and not first:
                                final_sums(j, 1, 2 * p - 1)
                            if k == 3:
                                if first and j == 0:
                                    pe.wait_ge(fin_weights, 1)
                                final_sums(j, 0, 2 * p)
                        if not first:
                            if k % 2 == 0 and t == 4:
                                layer1(2 * p - 2 + k // 2)
                            if k % 2 == 0 and t == 6:
                                layer2(2 * p - 2 + k // 2)
                            if k % 2 and t == 2:
                                layer3(2 * p - 2 + k // 2)

            pe.wait_ge(w1_split, 5)
            pe.wait_ge(fold_loaded, 16)
            for m in range(STEPS):
                for s in range(3):
                    for r in range(W1T):
                        mm = nc.tensor.matmul(spare[:, m * HID:(m + 1) * HID], fold[:, r, m * P:(m + 1) * P],
                                              w1_parts[:, s, r, :], start=(s == 0 and r == 0),
                                              stop=(s == 2 and r == W1T - 1))
            mm.then_inc(w_folded, 1)
            pe.wait_ge(consts_loaded, 32)
            for t in range(TILES):
                mm = nc.tensor.transpose(hidden[0:DENSE, t // 8, t // 4 % 2, (t % 4) * P:(t % 4 + 1) * P],
                                         dense_in[:, t, :], identf[:, :])
            mm.then_inc(dense_turned, 1)
            pe.wait_ge(dense_ready, 1)
            pe.wait_ge(w_ready, 2)
            pair_body(0, True)
            pe.wait_ge(mlp_loaded, 16 * 7)
            with pe.Fori(1, PAIRS) as p:
                pair_body(p, False)
            for j in range(len(GROUPS)):
                gram_group(3, j, 4 * PAIRS - 1)
                [layer1, layer2, layer3][j](TILES - 2)
            for j in range(3):
                final_sums(j, 1, TILES - 1)
            for layer in (layer1, layer2, layer3):
                layer(TILES - 1)
            pe.wait_ge(y_copied, TILES)
            nc.tensor.transpose(fin[0:TILES, 0:P], y_col[:, :], identf[:, :]).then_inc(y_turned, 1)

        @block.scalar
        def _(act):
            def sort_hidden(k, chunk):
                act.wait_ge(hid_first, chunk + 1)
                if not (isinstance(chunk, int) and chunk == 0):
                    act.wait_ge(hid_turned, 2 * chunk - 1)
                for bank in range(2):
                    if bank:
                        act.wait_ge(hid_steps, STEPS * (chunk + 1))
                    for c in range(2):
                        q, other = 2 * c + bank, 2 * c + 1 - bank
                        op = nc.scalar.activation(hid_high[32 * q:32 * q + 32, :],
                                                  hidden[32 * other:32 * other + 32, k % 2, bank, :], ACT.Copy)
                op.then_inc(hid_sorted, 1)
                act.wait_ge(hid_sorted, 2 * chunk + 1)
                for q in (1, 3):
                    rows = slice(32 * q, 32 * q + 32)
                    op = nc.scalar.activation(hidden[rows, k % 2, 0, :], hidden[rows, k % 2, 1, :], ACT.Copy)
                op.then_inc(hid_sorted, 1)

            def square_last(k, chunk, p):
                act.wait_ge(turned[k % 2], turns(k, p))
                if not (isinstance(chunk, int) and chunk == 0):
                    act.wait_ge(hid_steps, STEPS * chunk)
                nc.scalar.activation(last[0:F, :], x_rows[k % 2][0:F, :], ACT.Square).then_inc(last_squared, 1)

            def spread_x(k, part, chunk, tile):
                places = slice(0, SPREAD) if part == 0 else slice(SPREAD, HALF)
                if part == 0 and k % 2 == 0:
                    act.wait_ge(xt_ready, tile + 1)
                if not (isinstance(chunk, int) and chunk == 0):
                    act.wait_ge(gram_filled, len(GROUPS) * (chunk - 1) + 2 + part)
                for q in range(Q):
                    rows = slice(32 * q, 32 * q + 32)
                    op = nc.scalar.activation(
                        xdiag[rows, places, q * F:(q + 1) * F],
                        gst[k // 2][rows, 2 * places.start + k % 2:2 * places.stop:2, HID:GS], ACT.Copy)
                op.then_inc(xdiag_ready, 1)

            def gram_copy(k, j, chunk, tile):
                act.wait_ge(gram_filled, len(GROUPS) * chunk + j + 1)
                if k % 2 == 0 and j == 0 and not (isinstance(tile, int) and tile < 2):
                    act.wait_ge(fin_done, tile - 1)
                n = GROUPS[j] * Q
                col = k % 2 * HALF * Q + 2 * sum(GROUPS[:j]) * Q
                col += k // 2 * P
                g = gram[:, :, 0:n * F].rearrange("p u (b i) -> p i u b", i=F)

                def copy(out, i, rows, last_copy=False):
                    op = nc.scalar.activation(out[:, :, col:col + 2 * n].rearrange("p h (u b) -> p h u b", u=2),
                                              g[rows, i], ACT.Copy)
                    if last_copy:
                        op.then_inc(gram_out, 1)

                copy(gram2[0:HID, :], slice(0, F, 2), slice(0, HID))
                copy(gram2[HID:P, 0:FH - 1], slice(1, F, 2), slice(0, HID))
                for c in range(4):
                    rows = slice(c * SLOT, (c + 1) * SLOT)
                    copy(gram1[rows, 0:len(range(c, F, 4))], slice(c, F, 4), slice(HID, HID + SLOT))
                    rows = slice(c * SLOT, c * SLOT + TOP)
                    copy(gram1[rows, F1A:F1A + len(range(c, TOP, 4))], slice(SLOT + c, F, 4),
                         slice(HID + SLOT, GS), last_copy=(c == 3))

            def fin_half_copy(tile):
                act.wait_ge(fin_done, tile + 1)
                nc.scalar.activation(fin_half[:, :], fin_final1[64:128, :], ACT.Copy).then_inc(fin_half_out, 1)

            def relu1(tile):
                act.wait_ge(l1_done, tile + 1)
                for m in range(T1 // P):
                    op = nc.scalar.activation(act1[:, m, :], outs1[:, m, :], ACT.Relu, bias=bias1[:, m:m + 1])
                op.then_inc(l1_act, 1)

            def relu2(tile):
                act.wait_ge(l2_done, tile + 1)
                for m in range(T2 // P):
                    op = nc.scalar.activation(act2[:, m, :], outs2[:, m, :], ACT.Relu, bias=bias2[:, m:m + 1])
                op.then_inc(l2_act, 1)

            def pair_body(p, first):
                for k in range(4):
                    chunk = 4 * p + k
                    for t in range(STEPS):
                        if k % 2 == 0 and not first:
                            if t == 0:
                                fin_half_copy(2 * p - 2 + k // 2)
                            if t == 5:
                                relu1(2 * p - 2 + k // 2)
                        if t == 0:
                            square_last(k, chunk, p)
                        if t == STEPS - 1:
                            sort_hidden(k, chunk)
                        if t in (2, 4, 6) and (k or not first):
                            gram_copy((k - 1) % 4, t // 2 - 1, chunk - 1, 2 * p + (k - 1) // 2)
                        if t in (4, 6):
                            spread_x(k, t // 2 - 2, chunk, 2 * p + k // 2)
                        if t == 6 and k % 2 == 0 and not first:
                            relu2(2 * p - 2 + k // 2)

            act.wait_ge(cleared, 4)
            pair_body(0, True)
            act.wait_ge(mlp_loaded, 16 * 7)
            with act.Fori(1, PAIRS) as p:
                pair_body(p, False)
            fin_half_copy(TILES - 2)
            gram_copy(3, 0, 4 * PAIRS - 1, TILES - 1)
            relu1(TILES - 2)
            gram_copy(3, 1, 4 * PAIRS - 1, TILES - 1)
            relu2(TILES - 2)
            gram_copy(3, 2, 4 * PAIRS - 1, TILES - 1)
            fin_half_copy(TILES - 1)
            relu1(TILES - 1)
            relu2(TILES - 1)

        @block.vector
        def _(dve):
            def turn_x(tile, u, times):
                gathered_all(dve, u, times)
                if not (isinstance(tile, int) and tile < 2):
                    dve.wait_ge(gram_filled, 2 * len(GROUPS) * (tile - 1))
                nc.vector.transpose(gst[u][:, :, HID:GS].rearrange("p r f -> p f r"),
                                    emb[u][:, :].rearrange("p (f d) -> p f d", d=D)).then_inc(xt_ready, 1)

            def multiply(k, t, chunk, p):
                if t == STEPS - 1:
                    dve.wait_ge(last_moved, 16 * (chunk + 1))
                    rows = slice(LAST_AT, LAST_AT + F)
                    nc.vector.tensor_tensor(last[rows, :], x_rows[k % 2][rows, :], last[rows, :],
                                            ALU.mult).then_inc(multiplied, 1)
                    return
                if t < 3:
                    n = 3 * k + t
                    dve.wait_ge(moved[n % CRING], 16 * THIRDS * (3 * p + n // CRING + 1))
                if t == 0:
                    dve.wait_ge(tripled[k % 2], triples(k, p))
                if not (isinstance(chunk, int) and 6 * chunk + t < ZRING):
                    back = STEPS * chunk + t - ZRING + 1 if t >= ZRING else STEPS * (chunk - 1) + t + 6 - ZRING + 1
                    dve.wait_ge(hid_steps, back)

                def copy(u):
                    return x_moved[(3 * k + u - 1) % CRING][0:ROWS, :] if u else x_rows[k % 2][:, :]

                u, v = PRODUCTS[t]
                nc.vector.tensor_tensor(blocks[0:ROWS, (6 * k + t) % ZRING, :], copy(u), copy(v),
                                        ALU.mult).then_inc(multiplied, 1)

            def turn_hidden(k, chunk):
                for high in (1, 0):
                    dve.wait_ge(hid_sorted, 2 * chunk + 2 - high)
                    if high and not (isinstance(chunk, int) and chunk < 4):
                        dve.wait_ge(gram_filled, len(GROUPS) * (chunk - 3))
                    source = hid_high[:, :] if high else hidden[:, k % 2, 0, :]
                    nc.vector.transpose(gst[k // 2][:, k % 2::2, high * HALF_HID:high * HALF_HID + HALF_HID],
                                        source.rearrange("p (r d) -> p r d", d=D)).then_inc(hid_turned, 1)

            def final_copy(tile):
                dve.wait_ge(fin_half_out, tile + 1)
                nc.vector.tensor_tensor(z_rest[0:FIN1, :], fin_final1[0:FIN1, :], fin_half[:, :],
                                        ALU.add).then_inc(fin_out, 1)
                nc.vector.tensor_scalar(z_conv2[:, :], fin_conv2, 1.0, None, ALU.mult).then_inc(fin_out, 1)
                nc.vector.tensor_scalar(z_rest[FIN1:FIN1 + DENSE, :],
                                        dense_rows[FIN1:FIN1 + DENSE, bass.ds(tile * P, P)], 1.0, None,
                                        ALU.mult).then_inc(fin_out, 1)

            def y_copy(tile):
                dve.wait_ge(y_done, tile + 1)
                nc.vector.tensor_scalar(y_col[:, bass.ds(tile, 1)], spare[:, 0:1], 1.0, None,
                                        ALU.mult).then_inc(y_copied, 1)

            def pair_body(p, first, last_pair):
                for k in range(4):
                    chunk = 4 * p + k
                    for t in range(STEPS):
                        kk, tt = (k, t + AHEAD) if t + AHEAD < STEPS else (k + 1, t + AHEAD - STEPS)
                        if not (last_pair and kk == 4):
                            multiply(kk, tt, 4 * p + kk, p)
                        if t == 0 and (k or not first):
                            turn_hidden((k - 1) % 4, chunk - 1)
                        if t == 3 and k % 2 == 0:
                            turn_x(2 * p + k // 2, k // 2, p + 1)
                        if t == 1 and k % 2 == 0 and not first:
                            final_copy(2 * p - 2 + k // 2)
                        if t == 3 and k % 2 and not first:
                            y_copy(2 * p - 2 + k // 2)

            nc.vector.memset(w1_in[96:P, W1T - 1, :], 0.0).then_inc(zeroed, 1)
            nc.vector.memset(w_fin2[:, FH - 1, :], 0.0).then_inc(zeroed, 1)
            nc.vector.memset(w_fin1[:, :, :], 0.0).then_inc(zeroed, 1)
            nc.vector.memset(w_swapped[:, :, :], 0.0).then_inc(zeroed, 1)
            nc.vector.memset(xdiag[:, :, :], 0.0).then_inc(cleared, 1)
            dve.wait_ge(w1_loaded, 32)
            nc.vector.tensor_copy(w1_parts[:, 0], w1_in).then_inc(w1_split, 1)
            dve.wait_ge(w1_split, 1)
            nc.vector.tensor_tensor(w1_rem, w1_in, w1_parts[:, 0], ALU.subtract).then_inc(w1_split, 1)
            dve.wait_ge(w1_split, 2)
            nc.vector.tensor_copy(w1_parts[:, 1], w1_rem).then_inc(w1_split, 1)
            dve.wait_ge(w1_split, 3)
            nc.vector.tensor_tensor(w1_in, w1_rem, w1_parts[:, 1], ALU.subtract).then_inc(w1_split, 1)
            dve.wait_ge(w1_split, 4)
            nc.vector.tensor_copy(w1_parts[:, 2], w1_in).then_inc(w1_split, 1)
            dve.wait_ge(w_folded, 1)
            folded = spare[:, 0:STEPS * HID].rearrange("p (m k) -> p m k", k=HID)
            nc.vector.tensor_copy(w_pairs[:, :, 0:HID], folded).then_inc(w_ready, 1)
            nc.vector.tensor_copy(w_pairs[:, :, HID:], folded[:, :, 0:HALF_HID]).then_inc(w_ready, 1)
            dve.wait_ge(dense_turned, 1)
            for t in range(TILES):
                op = nc.vector.tensor_copy(
                    dense_rows[FIN1:FIN1 + DENSE, t * P:(t + 1) * P].rearrange("p (h r q) -> p q r h", h=2, q=Q),
                    hidden[0:DENSE, t // 8, t // 4 % 2, (t % 4) * P:(t % 4 + 1) * P].rearrange("p (q r h) -> p q r h", q=Q, h=2))
            op.then_inc(dense_ready, 1)
            dve.wait_ge(w1_split, 5)
            nc.vector.memset(arena[:, 0:FH * 2 * P], 0.0).then_inc(cleared, 1)
            nc.vector.memset(arena[:, FH * 2 * P:], 0.0).then_inc(cleared, 1)
            nc.vector.memset(last[:, :], 0.0).then_inc(cleared, 1)
            dve.wait_ge(fin_loaded, 16 * 14)
            nc.vector.tensor_tensor(w_fin1[:, F1A - F1B:F1A, :], w_fin1[:, F1A - F1B:F1A, :], w_swapped[:, :, :],
                                    ALU.add).then_inc(fin_weights, 1)
            for t in range(AHEAD):
                multiply(0, t, 0, 0)
            pair_body(0, True, False)
            with dve.Fori(1, PAIRS - 1) as p:
                pair_body(p, False, False)
            pair_body(PAIRS - 1, False, True)
            turn_hidden(3, 4 * PAIRS - 1)
            final_copy(TILES - 2)
            y_copy(TILES - 2)
            final_copy(TILES - 1)
            y_copy(TILES - 1)
            dve.wait_ge(y_turned, 1)
            nc.vector.tensor_copy(y_row[:, :].rearrange("t (q r h) -> t q r h", q=Q, h=2),
                                  fin[0:TILES, 0:P].rearrange("t (h r q) -> t q r h", h=2, q=Q)).then_inc(y_ready, 1)


def constants():
    import numpy as np

    fold = np.zeros((W1T * P, STEPS * P), "bfloat16")

    def pair(i, j, column):
        fold[i * F + j, column] = fold[j * F + i, column] = 1

    for t, (u, v) in enumerate(PRODUCTS):
        for g in range(THIRDS):
            for i in range(F):
                pair((i + ROTATION[u][g]) % F, (i + ROTATION[v][g]) % F, t * P + g * F + i)
    for i in range(F):
        pair(i, i, (STEPS - 1) * P + i)
        pair((LAST_SHIFT + i) % F, (LAST_SHIFT + i + LEFT) % F, (STEPS - 1) * P + LAST_AT + i)
    fold = np.ascontiguousarray(fold.reshape(W1T, P, STEPS * P).transpose(1, 0, 2))
    return fold, np.eye(P, dtype="float32")


def kernel(**inputs):
    import numpy as np
    import concourse.bacc as bacc
    from concourse.bass_utils import run_bass_kernel_spmd

    nc = bacc.Bacc("TRN2", target_bir_lowering=False, num_devices=1)
    fold, identf = constants()
    arrays = {n: np.ascontiguousarray(inputs[n]) for n in
              ["dense_ctx", "ids", *[f"tbl_{f}" for f in range(F)], "W_top1", "b_top1", "W_top2", "b_top2",
               "W_top3", "L0_rec_W1", "L0_rec_W2"]}
    arrays |= {"fold": fold, "identf": identf}
    arrays = {f"in_{n}": a for n, a in arrays.items()}
    d = {n: nc.dram_tensor(n, a.shape, mybir.dt.from_np(a.dtype), kind="ExternalInput").ap()
         for n, a in arrays.items()}
    y = nc.dram_tensor("out_y", (B, 1), F32, kind="ExternalOutput").ap()
    turning = nc.dram_tensor("turning", (2, P, F * D), F32, kind="Internal").ap()
    build(nc, d["in_dense_ctx"], d["in_ids"], [d[f"in_tbl_{f}"] for f in range(F)], d["in_W_top1"], d["in_b_top1"],
          d["in_W_top2"], d["in_b_top2"], d["in_W_top3"], d["in_L0_rec_W1"], d["in_L0_rec_W2"],
          d["in_fold"], d["in_identf"], turning, y)
    r = run_bass_kernel_spmd(nc, [arrays], core_ids=[0])
    return r.results[0]["out_y"]
```
